# Optimizing a Trainium2 kernel written in Bass

```python
import numpy as np
import jax
import jax.numpy as jnp

def _softmax(x, axis=-1):
    return jax.nn.softmax(x, axis=axis)

def _gelu(x):
    return jax.nn.gelu(x, approximate=True)

def _silu(x):
    return jax.nn.silu(x)

def _sigmoid(x):
    return jax.nn.sigmoid(x)

def _layernorm(x, axis=-1, eps=1e-05):
    m = jnp.mean(x, axis=axis, keepdims=True)
    v = jnp.var(x, axis=axis, keepdims=True)
    return (x - m) / jnp.sqrt(v + eps)

def _scatter_add(tgt, idx, src, axis=0):
    return tgt.at[idx].add(src)

def _segment_sum(src, seg, n):
    return jax.ops.segment_sum(src, seg, n)
kernel_name = 'mk_prb_d1_jaxref_r8_8f3465'

def setup_inputs(seed: int=0):
    np.random.seed(seed)
    _w = jnp.asarray

    def _L0_attn_setup():
        import jax, jax.numpy as jnp
        import numpy as np
        B, L, D, H, W = (2, 512, 128, 16, 128)
        E = D // H

        def _ln(x, g, b):
            m = jnp.mean(x, axis=-1, keepdims=True)
            v = jnp.mean((x - m) ** 2, axis=-1, keepdims=True)
            return (x - m) / jnp.sqrt(v + 1e-05) * g + b

        def _swa(xn, Wqkv, bqkv, Wp, bp):
            b_, l_, d_ = xn.shape
            nb = l_ // W
            qkv = xn @ Wqkv + bqkv
            q, k, v = jnp.split(qkv, 3, axis=-1)

            def heads(t):
                return t.reshape(b_, l_, H, E).transpose(0, 2, 1, 3)
            q, k, v = (heads(q), heads(k), heads(v))

            def blk(t):
                return t.reshape(b_, H, nb, W, E)
            qb, kb, vb = (blk(q), blk(k), blk(v))
            kprev = jnp.pad(kb, ((0, 0), (0, 0), (1, 0), (0, 0), (0, 0)))[:, :, :nb]
            vprev = jnp.pad(vb, ((0, 0), (0, 0), (1, 0), (0, 0), (0, 0)))[:, :, :nb]
            kc = jnp.concatenate([kprev, kb], axis=3)
            vc = jnp.concatenate([vprev, vb], axis=3)
            scores = jnp.einsum('bhnre,bhnse->bhnrs', qb, kc) / np.float32(np.sqrt(E))
            r = jnp.arange(W)[:, None]
            s = jnp.arange(2 * W)[None, :]
            band = (s >= r + 1) & (s <= r + W)
            first = band & (s >= W)
            mask = jnp.concatenate([first[None], jnp.broadcast_to(band, (nb - 1, W, 2 * W))], axis=0)
            scores = jnp.where(mask[None, None], scores, jnp.float32(-1e+30))
            attn = jax.nn.softmax(scores, axis=-1)
            out = jnp.einsum('bhnrs,bhnse->bhnre', attn, vc)
            out = out.reshape(b_, H, l_, E).transpose(0, 2, 1, 3).reshape(b_, l_, d_)
            return out @ Wp + bp

        def _linattn(xn, Wqkv, bqkv, Wo, bo):
            b_, l_, d_ = xn.shape
            C = 128
            nc = l_ // C
            qkv = xn @ Wqkv + bqkv
            q, k, v = jnp.split(qkv, 3, axis=-1)
            q = q.reshape(b_, l_, H, E)
            k = k.reshape(b_, l_, H, E)
            v = v.reshape(b_, l_, H, E)
            q = jax.nn.elu(q * np.float32(E ** (-0.5))) + np.float32(1.0001)
            k = jax.nn.elu(k) + np.float32(1.0001)

            def chunks(t):
                return t.reshape(b_, nc, C, H, E).transpose(1, 0, 3, 2, 4)
            qc, kc, vc = (chunks(q), chunks(k), chunks(v))
            tril = jnp.tril(jnp.ones((C, C), jnp.float32))

            def step(carry, inp):
                S, z = carry
                qi, ki, vi = inp
                A = jnp.einsum('bhce,bhde->bhcd', qi, ki) * tril
                num = jnp.einsum('bhce,bhef->bhcf', qi, S) + jnp.einsum('bhcd,bhdf->bhcf', A, vi)
                den = jnp.einsum('bhce,bhe->bhc', qi, z) + A.sum(-1)
                o = num / (den[..., None] + 1e-06)
                S = S + jnp.einsum('bhce,bhcf->bhef', ki, vi)
                z = z + ki.sum(2)
                return ((S, z), o)
            S0 = jnp.zeros((b_, H, E, E), jnp.float32)
            z0 = jnp.zeros((b_, H, E), jnp.float32)
            _, out = jax.lax.scan(step, (S0, z0), (qc, kc, vc))
            out = out.transpose(1, 0, 3, 2, 4).reshape(b_, l_, d_)
            return out @ Wo + bo
        key = jax.random.key(seed)
        ks = jax.random.split(key, 9)

        def w(k, shape, s=0.02):
            return jax.random.normal(k, shape, jnp.float32) * s
        return {'x': jax.random.normal(ks[0], (B, L, D), jnp.float32), 'g1': jnp.ones((D,), jnp.float32), 'b1': jnp.zeros((D,), jnp.float32), 'Wqkv_a': w(ks[1], (D, 3 * D)), 'bqkv_a': jnp.zeros((3 * D,), jnp.float32), 'Wp_a': w(ks[2], (D, D)), 'bp_a': jnp.zeros((D,), jnp.float32), 'Wqkv_s': w(ks[3], (D, 3 * D)), 'bqkv_s': jnp.zeros((3 * D,), jnp.float32), 'Wo_s': w(ks[4], (D, D)), 'bo_s': jnp.zeros((D,), jnp.float32), 'Wo': w(ks[5], (D, D)), 'bo': jnp.zeros((D,), jnp.float32), 'gm': jnp.ones((D,), jnp.float32), 'bm': jnp.zeros((D,), jnp.float32), 'W1': w(ks[6], (D, 4 * D)), 'b1m': jnp.zeros((4 * D,), jnp.float32), 'W2': w(ks[7], (4 * D, D)), 'b2m': jnp.zeros((D,), jnp.float32)}
    _L0_attn_in = _L0_attn_setup()

    def _L0_ffn_setup():
        import jax, jax.numpy as jnp
        import numpy as np
        FP8_E4M3_MAX = 448.0

        def fake_quant_fp8(t):
            amax = jnp.max(jnp.abs(t))
            scale = FP8_E4M3_MAX / jnp.maximum(amax, 1e-12)
            q = (t * scale).astype(jnp.float8_e4m3fn).astype(jnp.float32)
            return q / scale
        key = jax.random.key(seed)
        k1, k2, k3 = jax.random.split(key, 3)
        d_in, d_out = (128, 128)
        x = jax.random.normal(k1, (4, 1024, d_in), dtype=jnp.float32)
        weight = jax.random.normal(k2, (d_out, d_in), dtype=jnp.float32) * (1.0 / np.sqrt(d_in))
        bias = jax.random.normal(k3, (d_out,), dtype=jnp.float32) * 0.01
        return {'x': x, 'weight': weight, 'bias': bias}
    _L0_ffn_in = _L0_ffn_setup()
    _d = {'L0_attn_x': _L0_attn_in['x'], 'L0_attn_g1': _L0_attn_in['g1'], 'L0_attn_b1': _L0_attn_in['b1'], 'L0_attn_Wqkv_a': _L0_attn_in['Wqkv_a'], 'L0_attn_bqkv_a': _L0_attn_in['bqkv_a'], 'L0_attn_Wp_a': _L0_attn_in['Wp_a'], 'L0_attn_bp_a': _L0_attn_in['bp_a'], 'L0_attn_Wqkv_s': _L0_attn_in['Wqkv_s'], 'L0_attn_bqkv_s': _L0_attn_in['bqkv_s'], 'L0_attn_Wo_s': _L0_attn_in['Wo_s'], 'L0_attn_bo_s': _L0_attn_in['bo_s'], 'L0_attn_Wo': _L0_attn_in['Wo'], 'L0_attn_bo': _L0_attn_in['bo'], 'L0_attn_gm': _L0_attn_in['gm'], 'L0_attn_bm': _L0_attn_in['bm'], 'L0_attn_W1': _L0_attn_in['W1'], 'L0_attn_b1m': _L0_attn_in['b1m'], 'L0_attn_W2': _L0_attn_in['W2'], 'L0_attn_b2m': _L0_attn_in['b2m'], 'L0_ffn_weight': _L0_ffn_in['weight'], 'L0_ffn_bias': _L0_ffn_in['bias']}
    _x0 = _d['L0_attn_x']
    _d['L0_attn_x'] = jax.random.normal(jax.random.fold_in(jax.random.key(seed), 1), (4, 512, 128), dtype=_x0.dtype)
    del _x0
    return _d

def reference(L0_attn_x, L0_attn_g1, L0_attn_b1, L0_attn_Wqkv_a, L0_attn_bqkv_a, L0_attn_Wp_a, L0_attn_bp_a, L0_attn_Wqkv_s, L0_attn_bqkv_s, L0_attn_Wo_s, L0_attn_bo_s, L0_attn_Wo, L0_attn_bo, L0_attn_gm, L0_attn_bm, L0_attn_W1, L0_attn_b1m, L0_attn_W2, L0_attn_b2m, L0_ffn_weight, L0_ffn_bias):

    def _L0_attn_ref(x, g1, b1, Wqkv_a, bqkv_a, Wp_a, bp_a, Wqkv_s, bqkv_s, Wo_s, bo_s, Wo, bo, gm, bm, W1, b1m, W2, b2m):
        import jax, jax.numpy as jnp
        import numpy as np
        B, L, D, H, W = (2, 512, 128, 16, 128)
        E = D // H

        def _ln(x, g, b):
            m = jnp.mean(x, axis=-1, keepdims=True)
            v = jnp.mean((x - m) ** 2, axis=-1, keepdims=True)
            return (x - m) / jnp.sqrt(v + 1e-05) * g + b

        def _swa(xn, Wqkv, bqkv, Wp, bp):
            b_, l_, d_ = xn.shape
            nb = l_ // W
            qkv = xn @ Wqkv + bqkv
            q, k, v = jnp.split(qkv, 3, axis=-1)

            def heads(t):
                return t.reshape(b_, l_, H, E).transpose(0, 2, 1, 3)
            q, k, v = (heads(q), heads(k), heads(v))

            def blk(t):
                return t.reshape(b_, H, nb, W, E)
            qb, kb, vb = (blk(q), blk(k), blk(v))
            kprev = jnp.pad(kb, ((0, 0), (0, 0), (1, 0), (0, 0), (0, 0)))[:, :, :nb]
            vprev = jnp.pad(vb, ((0, 0), (0, 0), (1, 0), (0, 0), (0, 0)))[:, :, :nb]
            kc = jnp.concatenate([kprev, kb], axis=3)
            vc = jnp.concatenate([vprev, vb], axis=3)
            scores = jnp.einsum('bhnre,bhnse->bhnrs', qb, kc) / np.float32(np.sqrt(E))
            r = jnp.arange(W)[:, None]
            s = jnp.arange(2 * W)[None, :]
            band = (s >= r + 1) & (s <= r + W)
            first = band & (s >= W)
            mask = jnp.concatenate([first[None], jnp.broadcast_to(band, (nb - 1, W, 2 * W))], axis=0)
            scores = jnp.where(mask[None, None], scores, jnp.float32(-1e+30))
            attn = jax.nn.softmax(scores, axis=-1)
            out = jnp.einsum('bhnrs,bhnse->bhnre', attn, vc)
            out = out.reshape(b_, H, l_, E).transpose(0, 2, 1, 3).reshape(b_, l_, d_)
            return out @ Wp + bp

        def _linattn(xn, Wqkv, bqkv, Wo, bo):
            b_, l_, d_ = xn.shape
            C = 128
            nc = l_ // C
            qkv = xn @ Wqkv + bqkv
            q, k, v = jnp.split(qkv, 3, axis=-1)
            q = q.reshape(b_, l_, H, E)
            k = k.reshape(b_, l_, H, E)
            v = v.reshape(b_, l_, H, E)
            q = jax.nn.elu(q * np.float32(E ** (-0.5))) + np.float32(1.0001)
            k = jax.nn.elu(k) + np.float32(1.0001)

            def chunks(t):
                return t.reshape(b_, nc, C, H, E).transpose(1, 0, 3, 2, 4)
            qc, kc, vc = (chunks(q), chunks(k), chunks(v))
            tril = jnp.tril(jnp.ones((C, C), jnp.float32))

            def step(carry, inp):
                S, z = carry
                qi, ki, vi = inp
                A = jnp.einsum('bhce,bhde->bhcd', qi, ki) * tril
                num = jnp.einsum('bhce,bhef->bhcf', qi, S) + jnp.einsum('bhcd,bhdf->bhcf', A, vi)
                den = jnp.einsum('bhce,bhe->bhc', qi, z) + A.sum(-1)
                o = num / (den[..., None] + 1e-06)
                S = S + jnp.einsum('bhce,bhcf->bhef', ki, vi)
                z = z + ki.sum(2)
                return ((S, z), o)
            S0 = jnp.zeros((b_, H, E, E), jnp.float32)
            z0 = jnp.zeros((b_, H, E), jnp.float32)
            _, out = jax.lax.scan(step, (S0, z0), (qc, kc, vc))
            out = out.transpose(1, 0, 3, 2, 4).reshape(b_, l_, d_)
            return out @ Wo + bo
        xn = _ln(x, g1, b1)
        attn_out = _swa(xn, Wqkv_a, bqkv_a, Wp_a, bp_a)
        ssm_out = _linattn(xn, Wqkv_s, bqkv_s, Wo_s, bo_s)
        mixed = (attn_out + ssm_out) @ Wo + bo
        x1 = x + mixed
        h = _ln(x1, gm, bm)
        mlp = jax.nn.gelu(h @ W1 + b1m, approximate=False) @ W2 + b2m
        return x1 + mlp

    def _L0_ffn_ref(x, weight, bias):
        import jax, jax.numpy as jnp
        import numpy as np
        FP8_E4M3_MAX = 448.0

        def fake_quant_fp8(t):
            amax = jnp.max(jnp.abs(t))
            scale = FP8_E4M3_MAX / jnp.maximum(amax, 1e-12)
            q = (t * scale).astype(jnp.float8_e4m3fn).astype(jnp.float32)
            return q / scale
        xq = fake_quant_fp8(x)
        wq = fake_quant_fp8(weight)
        return jnp.einsum('bsd,od->bso', xq, wq) + bias
    x = L0_attn_x
    xn = _layernorm(x, axis=-1)
    x = x + _L0_attn_ref(xn, L0_attn_g1, L0_attn_b1, L0_attn_Wqkv_a, L0_attn_bqkv_a, L0_attn_Wp_a, L0_attn_bp_a, L0_attn_Wqkv_s, L0_attn_bqkv_s, L0_attn_Wo_s, L0_attn_bo_s, L0_attn_Wo, L0_attn_bo, L0_attn_gm, L0_attn_bm, L0_attn_W1, L0_attn_b1m, L0_attn_W2, L0_attn_b2m) + _L0_ffn_ref(xn, L0_ffn_weight, L0_ffn_bias)
    return x

_drawn_inputs = setup_inputs


def setup_inputs(seed=0):
    import zlib

    import numpy as np

    out = dict(_drawn_inputs(seed))
    spreads = {'L0_attn_g1': (1.0, 0.6),
     'L0_attn_b1': (0.0, 0.8),
     'L0_attn_bqkv_a': (0.0, 0.8),
     'L0_attn_bp_a': (0.0, 0.779),
     'L0_attn_bqkv_s': (0.0, 0.8),
     'L0_attn_bo_s': (0.0, 0.779),
     'L0_attn_bo': (0.0, 0.467),
     'L0_attn_gm': (1.0, 0.6),
     'L0_attn_bm': (0.0, 2.0),
     'L0_attn_b1m': (0.0, 0.78),
     'L0_attn_b2m': (0.0, 0.484)}
    factors = {'L0_attn_Wqkv_a': 8.0,
     'L0_attn_Wp_a': 8.0,
     'L0_attn_Wqkv_s': 8.0,
     'L0_attn_Wo_s': 8.0,
     'L0_attn_Wo': 3.685,
     'L0_ffn_bias': 33.008,
     'L0_attn_W1': 3.262}
    for name, (base, spread) in spreads.items():
        noise = np.random.default_rng([zlib.crc32(name.encode()), seed]).standard_normal(out[name].shape)
        drawn = base * np.exp(spread * noise) if base else spread * noise
        out[name] = jnp.asarray(drawn.astype(out[name].dtype))
    for name, factor in factors.items():
        out[name] = (out[name] * factor).astype(out[name].dtype)
    return out
```

```python
from contextlib import ExitStack

import concourse.bass as bass
from concourse import mybir

P = 128
H = 16
E = 8
C = 128
VW = 32
NPROD = 6
KROWS = NPROD * E
CROWS = 3
NEG = -1e30
LN_EPS = 1e-5
DEN_EPS = 1e-6
ELU_SHIFT = 1e-4
FP8_MAX = 448.0
AMAX_MIN = 1e-12
FP8_MIN_NORMAL = 2.0 ** -6
FP8_ROUND = 1.5 * 2.0 ** 20
EXPONENT_BITS = 0x7F800000

ALU = mybir.AluOpType
ACT = mybir.ActivationFunctionType
BF16 = mybir.dt.bfloat16
F32 = mybir.dt.float32
I32 = mybir.dt.int32
U32 = mybir.dt.uint32
AX_X = mybir.AxisListType.X

QA, KA, QS, KS = range(4)


def attention_block_kernel(nc, x, g1, b1, Wqkv_a, bqkv_a, Wp_a, bp_a, Wqkv_s, bqkv_s, Wo_s, bo_s,
                           Wo, bo, gm, bm, W1, b1m, W2, b2m, ffn_w, ffn_b, out):
    B, L, D = x.shape
    N = L // C
    F = W1.shape[1]
    FC = F // P
    SCALE = float(E) ** -0.5
    assert D == P and H * E == D and B % 2 == 0

    Q_PARTS = [0, 0, 0, 1, 1, 2]
    K_PARTS = [0, 1, 2, 0, 1, 0]
    PARTS = {QA: Q_PARTS, KA: K_PARTS, QS: Q_PARTS, KS: K_PARTS}

    SOFT = [(0, 0, 8), (0, 8, 8)] + [(m, 4 * g, 4) for m in range(1, N) for g in range(4)]
    NT = len(SOFT)
    LAST_TILE = {m: max(i for i, t in enumerate(SOFT) if t[0] == m) for m in range(N)}

    MISC = ["xT", "p0", "p1", "p2", "p3", "n0", "n1", "n2", "n3", "kv0", "kv1", "kv2", "cT",
            "l0nat", "l1nat", "l0T", "l2nat", "l1T", "l3nat", "l2T", "l3T"]
    MISC += ["s0nat", "s0T", "s1nat", "s1T", "s2nat", "s2T", "s3nat", "s3T", "mix"]
    NM = len(MISC)
    SLOT = {name: i for i, name in enumerate(MISC)}
    N_LIN = 2 * N
    SC_MAX, SC_LIN, SC_EXP = 0, NT, NT + N_LIN
    NSC = 2 * NT + N_LIN
    N_ACC = 2 * N
    PA = 4
    LAG = 3

    with ExitStack() as ctx:
        def sb(name, shape, dt=F32):
            return ctx.enter_context(nc.sbuf_tensor(name, shape, dt))

        def sem(name):
            return ctx.enter_context(nc.semaphore(name))

        ident = sb("ident", [P, P])
        ident16 = sb("ident16", [P, P], BF16)
        mask_win = sb("mask_win", [P, 2, 2, C], BF16)
        mask_first = sb("mask_first", [P, 4, C], BF16)
        causal = sb("causal", [P, C])
        own_head = sb("own_head", [P, H, E + 1])
        ones = sb("ones", [P, P])
        w_cols = sb("w_cols", [P, 4, P])
        w_nat = sb("w_nat", [P, 3 * P])
        wo = sb("wo", [P, P])
        w_mix = sb("w_mix", [P, 2, P])
        w1 = sb("w1", [P, F])
        w2 = sb("w2", [P, FC, P])
        wf = sb("wf", [P, P])
        wqT = sb("wqT", [P, P], BF16)
        cols = sb("cols", [P, 10])
        gb = sb("gb", [P, 4])
        b1c = sb("b1c", [P, FC])
        b_nat = sb("b_nat", [P, 3 * P])
        b_out = sb("b_out", [P, P])
        b_mix = sb("b_mix", [P, P])
        xn_all = sb("xn_all", [P, B, N, P])
        xh_all = sb("xh_all", [P, B, N, P])
        xq = sb("xq", [P, B, L], BF16)
        wq = sb("wq", [P, P], BF16)
        st_all = sb("st_all", [P, B, N, 6])
        xqT_all = sb("xqT_all", [P, B * N * P], BF16)
        st = sb("st", [P, N, 6])
        mv = sb("mv", [P, N, 2])
        var = sb("var", [P, N])
        sd = sb("sd", [P, N])
        rs = sb("rs", [P, N])
        rt = sb("rt", [P, N])
        mv2 = sb("mv2", [P, B * N, 2])
        var2 = sb("var2", [P, B * N])
        sd2 = sb("sd2", [P, B * N])
        rs2 = sb("rs2", [P, B * N])
        rt2 = sb("rt2", [P, B * N])
        am = sb("am", [P, 2])
        am1 = sb("am1", [1, 2])
        amb = sb("amb", [P, 2])
        fscale = sb("fscale", [P, 2])
        finv = sb("finv", [P, 2])
        dequant = sb("dequant", [P, 1])
        xh = sb("xh", [P, N, P])
        xT = sb("xT", [P, L])
        f = sb("f", [P, 4, L])
        parts = [sb(f"parts{i}", [P, 3, L], BF16) for i in range(4)]
        rest = sb("rest", [P, 4, L])
        stack = [sb(f"stack{i}", [64, H, L], BF16) for i in range(4)]
        v_a = sb("v_a", [P, N, H, VW])
        v_s = sb("v_s", [P, N, H, VW])
        k_lin = sb("k_lin", [P, L])
        phi = sb("phi", [P, 3, L])
        negc = sb("negc", [P, N, H])
        c_f = sb("c_f", [H, L])
        c_parts = sb("c_parts", [H, 3, L], BF16)
        kv_new = sb("kv_new", [P, H, E + 1])
        state = [sb(f"state{n}", [P, H, VW]) for n in range(1, N)]
        pa_all = sb("pa_all", [P, PA, 2 * 512])
        pa = [pa_all[:, i, :] for i in range(PA)]
        acc_s = [sb(f"acc_s{i}", [P, 512]) for i in range(2)]
        den = sb("den", [P, H])
        rden = sb("rden", [P, H])
        nat = [sb(f"nat{i}", [P, P]) for i in range(2)]
        oT = sb("oT", [P, 2, L])
        x_all = pa_all[:, 0:2, :].rearrange("p a (b n d) -> p (a b) n d", n=N, d=P)
        emin = pa_all[:, 0:2, :].rearrange("p a (c t) -> p (a c) t", t=L)
        x1_all = xh_all
        c_rest = rest[0:H, 0, :]
        wp = phi[:, 0, 0:2 * P].rearrange("p (a d) -> p a d", a=2)
        wpT = phi[:, 0, 2 * P:4 * P].rearrange("p (a d) -> p a d", a=2)
        pre = phi[:, 1, 0:P]
        bo_rows = phi[:, 1, P:2 * P]
        b_out2 = phi[:, 1, 2 * P:4 * P].rearrange("p (a d) -> p a d", a=2)
        hn = xh
        hT = xT
        hid = f
        r1 = phi[:, 0, :]
        r2 = phi[:, 1, :]
        r3 = phi[:, 2, :]
        o_sb = k_lin
        q_e = rest

        sc = [ctx.enter_context(nc.psum_tensor(f"sc{i}", [P, 1024], F32)) for i in range(2)]
        acc = [ctx.enter_context(nc.psum_tensor(f"acc{i}", [P, 512], F32)) for i in range(2)]
        misc = [ctx.enter_context(nc.psum_tensor(f"misc{i}", [P, 512], F32)) for i in range(2)]

        x_loaded = [sem(f"x_loaded{b}") for b in range(B)]
        w_loaded = sem("w_loaded")
        const_set = sem("const_set")
        const_ready = sem("const_ready")
        k_ones_set = sem("k_ones_set")
        dve_step = sem("dve_step")
        var_ready = sem("var_ready")
        sd_ready = sem("sd_ready")
        xh_ready = sem("xh_ready")
        amax_ready = sem("amax_ready")
        quant_ready = sem("quant_ready")
        pre_ready = sem("pre_ready")
        pre_full = sem("pre_full")
        pre_copied = sem("pre_copied")
        xh_loaded = sem("xh_loaded")
        xh_read = sem("xh_read")
        misc_full = sem("misc_full")
        misc_drained = [sem("misc_drained0"), sem("misc_drained1")]
        sc_full = sem("sc_full")
        sc_drained = [sem("sc_drained0"), sem("sc_drained1")]
        acc_full = sem("acc_full")
        acc_drained = [sem("acc_drained0"), sem("acc_drained1")]
        parts_ready = [sem(f"parts_ready{i}") for i in range(4)]
        scratch_written = [sem(f"scratch_written{i}") for i in range(4)]
        stacked = [sem(f"stacked{i}") for i in range(4)]
        c_ready = sem("c_ready")
        c_stacked = sem("c_stacked")
        min_ready = sem("min_ready")
        exp_ready = sem("exp_ready")
        phi_ready = sem("phi_ready")
        part1_ready = sem("part1_ready")
        rest_ready = sem("rest_ready")
        part2_ready = sem("part2_ready")
        state_ready = sem("state_ready")
        pa_used = sem("pa_used")
        tiles_taken = sem("tiles_taken")
        masked = sem("masked")
        x1_ready = sem("x1_ready")
        h_ready = sem("h_ready")
        amb_ready = sem("amb_ready")
        gelu_ready = sem("gelu_ready")
        resid_ready = sem("resid_ready")
        t2_ready = sem("t2_ready")
        out_ready = sem("out_ready")
        x_again = sem("x_again")
        stored = sem("stored")

        scratch = [nc.dram_tensor(f"scratch{i}", (P, 3, L), BF16, kind="Internal").ap() for i in range(4)]
        x_dram = x.rearrange("b (n p) d -> b p n d", p=P)
        out_dram = out.rearrange("b (n p) d -> b p n d", p=P)

        weights = [
            (w_cols[:, QA, :], Wqkv_a[:, 0:P]), (w_cols[:, KA, :], Wqkv_a[:, P:2 * P]),
            (w_cols[:, QS, :], Wqkv_s[:, 0:P]), (w_cols[:, KS, :], Wqkv_s[:, P:2 * P]),
            (w_nat[:, 0:P], Wqkv_a[:, 2 * P:3 * P]), (w_nat[:, P:2 * P], Wqkv_s[:, 2 * P:3 * P]),
            (w_nat[:, 2 * P:3 * P], Wqkv_s[:, P:2 * P]),
            (b_nat[:, 0:P], bqkv_a[2 * P:3 * P].partition_broadcast(P)),
            (b_nat[:, P:2 * P], bqkv_s[2 * P:3 * P].partition_broadcast(P)),
            (b_nat[:, 2 * P:3 * P], bqkv_s[P:2 * P].partition_broadcast(P)),
            (wp[:, 0, :], Wp_a), (wp[:, 1, :], Wo_s), (wo[:, :], Wo),
            (w1[:, :], W1), (w2[:, :, :], W2.rearrange("(k p) d -> p k d", p=P)), (wf[:, :], ffn_w),
            (bo_rows[:, :], bo.partition_broadcast(P)),
            (b_out2[:, 0, :], b2m.partition_broadcast(P)), (b_out2[:, 1, :], ffn_b.partition_broadcast(P)),
        ]
        columns = [(cols[:, 0:2], bqkv_a[0:2 * P]), (cols[:, 2:4], bqkv_s[0:2 * P]),
                   (cols[:, 4:5], g1), (cols[:, 5:6], b1), (cols[:, 6:7], gm), (cols[:, 7:8], bm),
                   (cols[:, 8:9], bp_a), (cols[:, 9:10], bo_s), (b1c[:, :], b1m)]
        W_ALL = 16 * (len(weights) + len(columns))
        CONST_ALL = 10
        PRE_FULL = 6

        def misc_of(name):
            return misc[SLOT[name] % 2]

        def wait_misc_full(eng, b, name):
            eng.wait_ge(misc_full, b * NM + SLOT[name] + 1)

        def wait_misc_drained(eng, b, name):
            eng.wait_ge(misc_drained[SLOT[name] % 2], b * (NM // 2) + SLOT[name] // 2 + 1)

        def wait_sc_drained(eng, b, u):
            eng.wait_ge(sc_drained[u % 2], b * (NSC // 2) + u // 2 + 1)

        def apart(eng):
            eng.wait_ge(w_loaded, W_ALL)

        block = ctx.enter_context(nc.Block())

        @block.sync
        def _(sp):
            for b in range(B):
                sp.dma_start(x_all[:, b, :, :], x_dram[b]).then_inc(x_loaded[b], 16)
            for dst, src in weights:
                sp.dma_start(dst, src).then_inc(w_loaded, 16)
            for dst, src in columns:
                sp.dma_start(dst, src.rearrange("(k p) -> p k", p=P), allow_slow_non_contiguous=True)\
                  .then_inc(w_loaded, 16)
            sp.wait_ge(k_ones_set, 1)
            with sp.Fori(0, B) as b:
                sp.wait_ge(xh_ready, b + 1)
                apart(sp)
                sp.wait_ge(xh_read, b)
                sp.dma_start(xh[:, :, :], xh_all[:, b, :, :]).then_inc(xh_loaded, 16)
                for pair in ((QA, KA), (KS, QS)):
                    for i in pair:
                        apart(sp)
                        sp.wait_ge(parts_ready[i], b + 1)
                        sp.wait_ge(stacked[i], 16 * NPROD * b)
                        sp.dma_start(scratch[i], parts[i][:, :, :]).then_inc(scratch_written[i], 16)
                    for i in pair:
                        sp.wait_ge(scratch_written[i], 16 * (b + 1))
                        for g, part in enumerate(PARTS[i]):
                            sp.dma_start(stack[i][g * E:(g + 1) * E, :, :],
                                         scratch[i][:, part, :].rearrange("(h e) t -> e h t", e=E))\
                              .then_inc(stacked[i], 16)
                apart(sp)
                sp.wait_ge(c_ready, b + 1)
                for r in range(CROWS):
                    sp.dma_start(stack[QA][KROWS + r:KROWS + r + 1, :, :], c_parts[:, r, :])\
                      .then_inc(c_stacked, 16)
            sp.wait_ge(misc_full, NM * B)
            with sp.Fori(0, B) as b:
                apart(sp)
                sp.wait_ge(out_ready, b)
                sp.dma_start(r3.rearrange("p (n d) -> p n d", d=P), x_dram[b]).then_inc(x_again, 16)
                apart(sp)
                sp.wait_ge(out_ready, b + 1)
                sp.dma_start(out_dram[b], o_sb[:, :].rearrange("p (n d) -> p n d", d=P)).then_inc(stored, 16)
            sp.wait_ge(stored, 16 * B)

        @block.gpsimd
        def _(pool):
            for tile, value in ((ident, 0.0), (ident16, 0.0), (mask_win, 0.0), (mask_first, 0.0),
                                (causal, 1.0), (own_head, 1.0), (v_a, 1.0), (v_s, 1.0),
                                (ones, 1.0)):
                pool.memset(tile[tuple(slice(None) for _ in tile.shape)], value).then_inc(const_set, 1)
            for s in state:
                pool.memset(s[:, :, :], 0.0).then_inc(const_set, 1)
            pool.wait_ge(const_set, 9 + len(state))
            for tile in (ident, ident16):
                pool.affine_select(out=tile[:, :], in_=tile[:, :], pattern=[[-1, P]], compare_op=ALU.not_equal,
                                   fill=1.0, base=0, channel_multiplier=1).then_inc(const_ready, 1)
            pool.affine_select(out=mask_win[:, :, 0, :], in_=mask_win[:, :, 0, :], pattern=[[0, 2], [1, C]],
                               compare_op=ALU.is_gt, fill=NEG, base=0, channel_multiplier=-1)\
                .then_inc(const_ready, 1)
            pool.affine_select(out=mask_win[:, :, 1, :], in_=mask_win[:, :, 1, :], pattern=[[0, 2], [-1, C]],
                               compare_op=ALU.is_ge, fill=NEG, base=0, channel_multiplier=1)\
                .then_inc(const_ready, 1)
            pool.affine_select(out=mask_first[:, :, :], in_=mask_first[:, :, :], pattern=[[0, 4], [-1, C]],
                               compare_op=ALU.is_ge, fill=NEG, base=0, channel_multiplier=1)\
                .then_inc(const_ready, 1)
            pool.affine_select(out=causal[:, :], in_=causal[:, :], pattern=[[1, C]], compare_op=ALU.is_ge,
                               fill=0.0, base=0, channel_multiplier=-1).then_inc(const_ready, 1)
            pool.affine_select(out=own_head[:, :, :], in_=own_head[:, :, :], pattern=[[-E, H], [0, E + 1]],
                               compare_op=ALU.is_ge, fill=0.0, base=0, channel_multiplier=1)\
                .then_inc(const_ready, 1)
            pool.wait_ge(const_ready, 7)
            pool.affine_select(out=own_head[:, :, :], in_=own_head[:, :, :], pattern=[[E, H], [0, E + 1]],
                               compare_op=ALU.is_ge, fill=0.0, base=E - 1, channel_multiplier=-1)\
                .then_inc(const_ready, 1)
            for v in (v_a, v_s):
                pool.memset(v[:, :, :, E + 1:VW], 0.0).then_inc(const_ready, 1)
            pool.wait_ge(const_ready, 10)
            pool.memset(stack[KA][32:64, :, :].rearrange("p h t -> p (h t)").bitcast(U32), 0x3F803F80)\
                .then_inc(k_ones_set, 1)
            pool.wait_ge(k_ones_set, 1)
            pool.wait_ge(w_loaded, W_ALL)
            pool.tensor_tensor(b_out[:, :], b_out2[:, 0, :], b_out2[:, 1, :], ALU.add).then_inc(const_ready, 1)

            with pool.Fori(0, B) as b:
                for j, i in enumerate((KS, QS)):
                    pool.wait_ge(part1_ready, 2 * b + j + 1)
                    pool.tensor_tensor(rest[:, i, :], phi[:, i - QS, :], parts[i][:, 0, :], ALU.subtract)\
                        .then_inc(rest_ready, 1)
                for j, i in enumerate((KS, QS)):
                    pool.wait_ge(part2_ready, 2 * b + j + 1)
                    pool.tensor_tensor(parts[i][:, 2, :], rest[:, i, :], parts[i][:, 1, :], ALU.subtract)\
                        .then_inc(parts_ready[i], 1)
                for i, (m, h0, nh) in enumerate(SOFT):
                    wait_sc_drained(pool, b, SC_EXP + i)
                    pool.sem_inc(tiles_taken, 1)
                    k = (N_LIN + i) % PA
                    if m == 0:
                        p = pa[k].rearrange("p (h r) -> p h r", r=C)
                        pool.affine_select(out=p, in_=p, pattern=[[0, nh], [1, C]], compare_op=ALU.is_ge,
                                           fill=0.0, base=0, channel_multiplier=-1).then_inc(masked, 1)
                    else:
                        p = pa[k].rearrange("p (h w r) -> p h w r", w=2, r=C)
                        pool.affine_select(out=p[:, :, 0, :], in_=p[:, :, 0, :], pattern=[[0, nh], [-1, C]],
                                           compare_op=ALU.is_gt, fill=0.0, base=0, channel_multiplier=1)
                        pool.affine_select(out=p[:, :, 1, :], in_=p[:, :, 1, :], pattern=[[0, nh], [1, C]],
                                           compare_op=ALU.is_ge, fill=0.0, base=0, channel_multiplier=-1)\
                            .then_inc(masked, 1)

            pool.wait_ge(misc_full, NM * B)
            with pool.Fori(0, B) as b:
                pool.wait_ge(x_again, 16 * (b + 1))
                pool.tensor_tensor(r3.rearrange("p (n d) -> p n d", d=P), r3.rearrange("p (n d) -> p n d", d=P),
                                   b_out[:, :].rearrange("p (a d) -> p a d", a=1).to_broadcast([P, N, P]),
                                   ALU.add).then_inc(resid_ready, 1)
                pool.wait_ge(resid_ready, b + 1)
                pool.wait_ge(t2_ready, b + 1)
                pool.wait_ge(stored, 16 * b)
                pool.tensor_tensor(o_sb[:, :], r2, r3, ALU.add).then_inc(out_ready, 1)

        @block.scalar
        def _(act):
            def sqrt(j, dst, src):
                act.wait_ge(var_ready, j)
                nc.scalar.activation(dst, src, ACT.Sqrt).then_inc(sd_ready, 1)

            for b in range(B):
                sqrt(2 * b + 1, sd[:, :], var[:, :])
                sqrt(2 * b + 2, sd[:, :], var[:, :])
            act.wait_ge(pre_full, 2)
            nc.scalar.activation(wpT[:, :, :], sc[0][:, 0:2 * P].rearrange("p (a d) -> p a d", a=2), ACT.Copy)\
                .then_inc(pre_copied, 1)
            act.wait_ge(pre_full, 4)
            nc.scalar.activation(w_mix[:, :, :], sc[1][:, 0:2 * P].rearrange("p (a d) -> p a d", a=2), ACT.Copy)\
                .then_inc(pre_copied, 1)

            with act.Fori(0, B) as b:
                def drain(name, dst, func=ACT.Copy, **kw):
                    wait_misc_full(act, b, name)
                    s = SLOT[name]
                    nc.scalar.activation(dst, kw.pop("src"), func, **kw).then_inc(misc_drained[s % 2], 1)

                drain("xT", xT[:, :], ACT.Identity, src=misc_of("xT")[:, :], scale=cols[:, 4:5], bias=cols[:, 5:6])
                for i in (QA, KA, QS, KS):
                    if i in (QA, QS):
                        for j in (QA, KA) if i == QA else ():
                            act.wait_ge(parts_ready[j], b)
                        if i == QS:
                            act.wait_ge(phi_ready, 3 * b)
                        drain(f"p{i}", f[:, i, :], ACT.Identity, src=misc_of(f"p{i}")[:, :],
                              scale=SCALE, bias=gb[:, i:i + 1])
                    else:
                        drain(f"p{i}", f[:, i, :], ACT.Identity, src=misc_of(f"p{i}")[:, :],
                              scale=1.0, bias=gb[:, i:i + 1])
                for j in range(3):
                    act.wait_ge(min_ready, 3 * b + j + 1)
                    nc.scalar.activation(emin[:, j, :], emin[:, j, :], ACT.Exp).then_inc(exp_ready, 1)
                for j, i in enumerate((KS, QS)):
                    act.wait_ge(phi_ready, 3 * b + j + 1)
                    act.wait_ge(scratch_written[i], 16 * b)
                    nc.scalar.activation(parts[i][:, 0, :], phi[:, i - QS, :], ACT.Copy).then_inc(part1_ready, 1)
                for j, i in enumerate((KS, QS)):
                    act.wait_ge(rest_ready, 2 * b + j + 1)
                    nc.scalar.activation(parts[i][:, 1, :], rest[:, i, :], ACT.Copy).then_inc(part2_ready, 1)
                drain("cT", c_f[:, :], src=misc_of("cT")[0:H, :])

                def save_acc(u):
                    if u < N:
                        act.wait_ge(acc_full, b * N + u + 1)
                    else:
                        act.wait_ge(pa_used, b * NT + LAST_TILE[u - N] + 1)
                    if u >= 2:
                        wait_misc_full(act, b, f"{'ls'[(u - 2) // N]}{(u - 2) % N}nat")
                    nc.scalar.activation(acc_s[u % 2][:, :], acc[u % 2][:, :], ACT.Copy)\
                        .then_inc(acc_drained[u % 2], 1)

                def save_T(u):
                    kind, n = u // N, u % N
                    name = f"{'ls'[kind]}{n}T"
                    drain(name, oT[:, kind, n * C:(n + 1) * C], src=misc_of(name)[:, 0:C])

                for n in range(N):
                    save_acc(n)
                    if n >= 2:
                        save_T(n - 2)
                save_T(2)
                for i in range(NT + 8):
                    if i < NT:
                        u = SC_EXP + i
                        act.wait_ge(sc_full, b * NSC + u + 1)
                        if i < PA:
                            act.wait_ge(acc_full, b * N + (N_LIN - PA + i) // 2 + 1)
                        else:
                            act.wait_ge(pa_used, b * NT + i - PA + 1)
                        nc.scalar.activation(pa[(N_LIN + i) % PA], sc[u % 2][:, :], ACT.Exp)\
                            .then_inc(sc_drained[u % 2], 1)
                    if i == 1:
                        save_T(3)
                    for m in range(N):
                        if i == LAST_TILE[m] + LAG + 1:
                            save_acc(N + m)
                        if i == LAST_TILE[m] + LAG + 5:
                            save_T(N + m)

            sqrt(2 * B + 1, sd2[:, :], var2[:, :])
            for t in range(4):
                act.wait_ge(pre_full, PRE_FULL + t + 1)
                nc.scalar.activation(xqT_all[:, t * 512:(t + 1) * 512],
                                     sc[t % 2][:, 0:256].bitcast(BF16), ACT.Copy).then_inc(pre_copied, 1)
            act.wait_ge(pre_full, PRE_FULL + 5)
            nc.scalar.activation(wqT[:, :], sc[0][:, 0:64].bitcast(BF16), ACT.Copy).then_inc(pre_copied, 1)
            with act.Fori(0, B) as b:
                m0 = NM * B
                act.wait_ge(misc_full, m0 + 6 * b + 1)
                nc.scalar.activation(hT[:, :], misc[0][:, :], ACT.Identity, scale=cols[:, 6:7], bias=cols[:, 7:8])\
                    .then_inc(misc_drained[0], 1)
                act.wait_ge(sc_full, NSC * B + b)
                for k in range(FC):
                    act.wait_ge(misc_full, m0 + 6 * b + 2 + k)
                    nc.scalar.activation(hid[:, k, :], misc[(1 + k) % 2][:, :], ACT.Gelu, bias=b1c[:, k:k + 1])\
                        .then_inc(misc_drained[(1 + k) % 2], 1)

        @block.vector
        def _(dve):
            done = [0]

            def step(ins, base=0):
                done[0] += 1
                ins.then_inc(dve_step, 1)
                dve.wait_ge(dve_step, base + done[0])

            def rsqrt(ve, root, r, t, j, base=0):
                dve.wait_ge(sd_ready, j)
                step(nc.vector.reciprocal(r, root), base)
                step(nc.vector.tensor_tensor(t, r, r, ALU.mult), base)
                step(nc.vector.tensor_tensor(t, t, ve, ALU.mult), base)
                step(nc.vector.tensor_scalar(t, t, -0.5, 1.5, ALU.mult, ALU.add), base)
                step(nc.vector.tensor_tensor(r, r, t, ALU.mult), base)

            for b in range(B):
                dve.wait_ge(x_loaded[b], 16)
                for k, (src, dst) in enumerate(((x_all, xn_all), (xn_all, xh_all))):
                    for n in range(N):
                        ins = nc.vector.bn_stats(st[:, n, :], src[:, b, n, :])
                    step(ins)
                    for n in range(N):
                        ins = nc.vector.bn_aggr(mv[:, n, :], st[:, n, :])
                    step(ins)
                    nc.vector.tensor_scalar(var[:, :], mv[:, :, 1], LN_EPS, None, ALU.add).then_inc(var_ready, 1)
                    rsqrt(var[:, :], sd[:, :], rs[:, :], rt[:, :], 2 * b + k + 1)
                    for n in range(N):
                        ins = nc.vector.tensor_scalar(dst[:, b, n, :], src[:, b, n, :], mv[:, n, 0:1],
                                                      rs[:, n:n + 1], ALU.subtract, ALU.mult)
                    if k == 0:
                        step(ins)
                    else:
                        ins.then_inc(xh_ready, 1)
            dve.wait_ge(w_loaded, W_ALL)
            step(nc.vector.tensor_scalar(gb[:, :], cols[:, 0:4], 1.0, None, ALU.mult))
            step(nc.vector.tensor_scalar(gb[:, 0:4:2], cols[:, 0:4:2], SCALE, None, ALU.mult))
            step(nc.vector.tensor_scalar(rt[:, 0:1], cols[:, 8:9], cols[:, 9:10], None, ALU.add))
            dve.wait_ge(const_ready, CONST_ALL)
            nc.vector.tensor_scalar(pre, ones[:, :], rt[:, 0:1], None, ALU.mult).then_inc(pre_ready, 1)
            nc.vector.tensor_reduce(am[:, 0:1], xn_all[:, :, :, :].rearrange("p b n d -> p (b n d)"), AX_X, ALU.max,
                                    apply_absolute_value=True)
            nc.vector.tensor_reduce(am[:, 1:2], wf[:, :], AX_X, ALU.max, apply_absolute_value=True)\
                .then_inc(amax_ready, 1)
            dve.wait_ge(pre_full, 5)
            step(nc.vector.tensor_tensor(b_mix[:, :], acc[0][:, 0:P], bo_rows[:, :], ALU.add))
            step(nc.vector.tensor_reduce(am1[:, :], acc[1][0:1, 0:2 * P].rearrange("p (a d) -> p a d", a=2),
                                         AX_X, ALU.max))
            nc.vector.tensor_scalar(am1[:, :], am1[:, :], AMAX_MIN, None, ALU.max).then_inc(amax_ready, 1)
            dve.wait_ge(pre_full, 6)
            nc.vector.tensor_copy(amb[:, :], acc[0][:, 0:2]).then_inc(amb_ready, 1)
            dve.wait_ge(amb_ready, 1)
            step(nc.vector.reciprocal(amb[:, :], amb[:, :]))
            step(nc.vector.tensor_scalar(fscale[:, :], amb[:, :], FP8_MAX, None, ALU.mult))
            step(nc.vector.reciprocal(finv[:, :], fscale[:, :]))
            step(nc.vector.tensor_tensor(dequant[:, :], finv[:, 0:1], finv[:, 1:2], ALU.mult))

            y, big = q_e[:, 0, :], q_e[:, 1, :]

            def quantise(dst, src, scale, w):
                step(nc.vector.tensor_scalar(y[:, 0:w], src, scale, None, ALU.mult))
                step(nc.vector.tensor_scalar(big[:, 0:w].bitcast(I32), y[:, 0:w].bitcast(I32),
                                             EXPONENT_BITS, None, ALU.bitwise_and))
                step(nc.vector.tensor_scalar(big[:, 0:w], big[:, 0:w], FP8_MIN_NORMAL, FP8_ROUND,
                                             ALU.max, ALU.mult))
                step(nc.vector.tensor_tensor(y[:, 0:w], y[:, 0:w], big[:, 0:w], ALU.add))
                step(nc.vector.tensor_tensor(dst, y[:, 0:w], big[:, 0:w], ALU.subtract))

            for t in range(B):
                quantise(xq[:, t, :], xn_all[:, t, :, :].rearrange("p n d -> p (n d)"), fscale[:, 0:1], L)
            quantise(wq[:, :], wf[:, :], fscale[:, 1:2], P)
            before = done[0]
            dve.wait_ge(const_ready, CONST_ALL + 1)
            BATCH_STEPS = 2 * 3 + 3 + 3 + 2 * N_ACC + 1
            done[0] = 0
            with dve.Fori(0, B) as b:
                base = before + b * BATCH_STEPS
                for i in (QA, KA):
                    wait_misc_drained(dve, b, f"p{i}")
                    dve.wait_ge(scratch_written[i], 16 * b)
                    step(nc.vector.tensor_copy(parts[i][:, 0, :], f[:, i, :]), base)
                    step(nc.vector.tensor_tensor(rest[:, i, :], f[:, i, :], parts[i][:, 0, :], ALU.subtract), base)
                    step(nc.vector.tensor_copy(parts[i][:, 1, :], rest[:, i, :]), base)
                    nc.vector.tensor_tensor(parts[i][:, 2, :], rest[:, i, :], parts[i][:, 1, :], ALU.subtract)\
                        .then_inc(parts_ready[i], 1)
                for n in range(N):
                    name = f"n{n}"
                    wait_misc_full(dve, b, name)
                    m = misc_of(name)
                    for v, o in ((v_a, 0), (v_s, P)):
                        nc.vector.tensor_tensor(v[:, n, :, 0:E], m[:, o:o + P].rearrange("p (h e) -> p h e", e=E),
                                                b_nat[:, o:o + P].rearrange("p (h e) -> p h e", e=E), ALU.add)
                    nc.vector.tensor_tensor(k_lin[:, n * C:(n + 1) * C], m[:, 2 * P:3 * P], b_nat[:, 2 * P:3 * P],
                                            ALU.add).then_inc(misc_drained[SLOT[name] % 2], 1)
                wait_misc_drained(dve, b, "p3")
                wait_misc_drained(dve, b, "n3")
                srcs = ((1, f[:, KS, :]), (0, f[:, QS, :]), (2, k_lin[:, :]))
                for c, (_, src) in enumerate(srcs):
                    nc.vector.tensor_scalar(emin[:, c, :], src, 0.0, None, ALU.min).then_inc(min_ready, 1)
                for _, src in srcs:
                    step(nc.vector.tensor_scalar(src, src, 0.0, ELU_SHIFT, ALU.max, ALU.add), base)
                for c, (j, src) in enumerate(srcs):
                    dve.wait_ge(exp_ready, 3 * b + c + 1)
                    nc.vector.tensor_tensor(phi[:, j, :], emin[:, c, :], src, ALU.add).then_inc(phi_ready, 1)
                for i, (m, h0, nh) in enumerate(SOFT):
                    u = SC_MAX + i
                    dve.wait_ge(sc_full, b * NSC + u + 1)
                    nc.vector.tensor_reduce(negc[:, m, h0:h0 + nh], sc[u % 2][:, :].rearrange("p (h s) -> p h s", h=nh),
                                            AX_X, ALU.max, negate=True).then_inc(sc_drained[u % 2], 1)

                def mask_lin(n):
                    for k in range(2):
                        t = 2 * n + k
                        u = SC_LIN + t
                        dve.wait_ge(sc_full, b * NSC + u + 1)
                        if t >= PA:
                            dve.wait_ge(acc_full, b * N + (t - PA) // 2 + 1)
                        nc.vector.tensor_tensor(
                            pa[t % PA].rearrange("p (h r) -> p h r", r=C),
                            sc[u % 2][:, :].rearrange("p (h r) -> p h r", r=C),
                            causal[:, :].rearrange("p (a r) -> p a r", a=1).to_broadcast([P, 8, C]), ALU.mult)\
                            .then_inc(sc_drained[u % 2], 1)

                mask_lin(0)
                mask_lin(1)
                for n in range(N - 1):
                    name = f"kv{n}"
                    wait_misc_full(dve, b, name)
                    m = misc_of(name)[:, 0:H * (E + 1)].rearrange("p (h f) -> p h f", h=H)
                    if n == 0:
                        nc.vector.tensor_tensor(state[0][:, :, 0:E + 1], m, own_head[:, :, :], ALU.mult)\
                            .then_inc(misc_drained[SLOT[name] % 2], 1)
                    else:
                        nc.vector.tensor_tensor(kv_new[:, :, :], m, own_head[:, :, :], ALU.mult)\
                            .then_inc(misc_drained[SLOT[name] % 2], 1)
                        wait_misc_drained(dve, b, name)
                        if n == 1:
                            wait_misc_drained(dve, b, "kv0")
                        nc.vector.tensor_tensor(state[n][:, :, 0:E + 1], state[n - 1][:, :, 0:E + 1],
                                                kv_new[:, :, :], ALU.add).then_inc(state_ready, 1)
                        dve.wait_ge(state_ready, 2 * b + n)
                wait_misc_drained(dve, b, "cT")
                dve.wait_ge(c_stacked, 16 * CROWS * b)
                step(nc.vector.tensor_copy(c_parts[:, 0, :], c_f[:, :]), base)
                step(nc.vector.tensor_tensor(c_rest, c_f[:, :], c_parts[:, 0, :], ALU.subtract), base)
                step(nc.vector.tensor_copy(c_parts[:, 1, :], c_rest), base)
                nc.vector.tensor_tensor(c_parts[:, 2, :], c_rest, c_parts[:, 1, :], ALU.subtract)\
                    .then_inc(c_ready, 1)

                def normalise(u):
                    kind, n = u // N, u % N
                    name = f"{'ls'[kind]}{n}nat"
                    wait_misc_full(dve, b, name)
                    m = misc_of(name)[:, :].rearrange("p (h f) -> p h f", f=VW)
                    step(nc.vector.tensor_scalar(den[:, :], m[:, :, E], 0.0 if kind else DEN_EPS, None, ALU.add), base)
                    step(nc.vector.reciprocal(rden[:, :], den[:, :]), base)
                    if u >= 2:
                        wait_misc_full(dve, b, f"{'ls'[(u - 2) // N]}{(u - 2) % N}T")
                    nc.vector.tensor_tensor(nat[u % 2][:, :].rearrange("p (h e) -> p h e", e=E), m[:, :, 0:E],
                                            rden[:, :].rearrange("p (h a) -> p h a", a=1).to_broadcast([P, H, E]),
                                            ALU.mult).then_inc(misc_drained[SLOT[name] % 2], 1)

                for n in range(N):
                    if n + 2 < N:
                        mask_lin(n + 2)
                    if n >= 1:
                        normalise(n - 1)
                normalise(N - 1)
                for n in range(N):
                    normalise(N + n)
                wait_misc_full(dve, b, "mix")
                step(nc.vector.tensor_tensor(x1_all[:, b, :, :],
                                             misc_of("mix")[:, :].rearrange("p (n d) -> p n d", d=P),
                                             xn_all[:, b, :, :], ALU.add), base)
                nc.vector.tensor_tensor(x1_all[:, b, :, :], x1_all[:, b, :, :],
                                        b_mix[:, :].rearrange("p (a d) -> p a d", a=1).to_broadcast([P, N, P]),
                                        ALU.add).then_inc(misc_drained[SLOT["mix"] % 2], 1)
            assert done[0] == BATCH_STEPS
            done[0] = before + B * BATCH_STEPS
            dve.wait_ge(misc_drained[SLOT["mix"] % 2], B * (NM // 2))
            for t in range(B * N):
                ins = nc.vector.bn_stats(st_all[:, t // N, t % N, :], x1_all[:, t // N, t % N, :])
            step(ins)
            for t in range(B * N):
                ins = nc.vector.bn_aggr(mv2[:, t, :], st_all[:, t // N, t % N, :])
            step(ins)
            nc.vector.tensor_scalar(var2[:, :], mv2[:, :, 1], LN_EPS, None, ALU.add).then_inc(var_ready, 1)
            rsqrt(var2[:, :], sd2[:, :], rs2[:, :], rt2[:, :], 2 * B + 1)
            with dve.Fori(0, B) as b:
                m0 = NM * B
                dve.wait_ge(misc_full, m0 + 6 * b - 5)
                for n in range(N):
                    ins = nc.vector.tensor_scalar(hn[:, n, :], x1_all[:, b, n, :], mv2[:, b * N + n, 0:1],
                                                  rs2[:, bass.ds(b * N + n, 1)], ALU.subtract, ALU.mult)
                ins.then_inc(h_ready, 1)
                dve.wait_ge(misc_full, m0 + 6 * b + 6)
                dve.wait_ge(out_ready, b)
                nc.vector.scalar_tensor_tensor(out=r1, in0=misc[1][:, :], scalar=dequant[:, 0:1],
                                               in1=x1_all[:, b, :, :].rearrange("p n d -> p (n d)"),
                                               op0=ALU.mult, op1=ALU.add).then_inc(misc_drained[1], 1)
                dve.wait_ge(misc_drained[1], B * (NM // 2) + 3 * b + 3)
                dve.wait_ge(sc_full, NSC * B + b + 1)
                nc.vector.tensor_tensor(r2, sc[0][:, 0:512], r1, ALU.add).then_inc(t2_ready, 1)

        @block.tensor
        def _(pe):
            pe.wait_ge(const_ready, CONST_ALL)
            pe.wait_ge(w_loaded, W_ALL)
            for k in range(2):
                nc.tensor.transpose(sc[0][:, k * P:(k + 1) * P], wp[:, k, :], ident[:, :]).then_inc(pre_full, 1)
            pe.wait_ge(pre_copied, 1)
            for k in range(2):
                nc.tensor.matmul(sc[1][:, k * P:(k + 1) * P], wpT[:, k, :], wo[:, :], start=True, stop=True)\
                    .then_inc(pre_full, 1)
            pe.wait_ge(pre_ready, 1)
            nc.tensor.matmul(acc[0][:, 0:P], pre, wo[:, :], start=True, stop=True)
            pe.wait_ge(amax_ready, 1)
            nc.tensor.transpose(acc[1][0:1, 0:P], am[:, 0:1], ident[:, :])
            nc.tensor.transpose(acc[1][0:1, P:2 * P], am[:, 1:2], ident[:, :]).then_inc(pre_full, 1)
            pe.wait_ge(amax_ready, 2)
            nc.tensor.matmul(acc[0][:, 0:2], ones[0:1, :], am1[:, :], start=True, stop=True).then_inc(pre_full, 1)
            pe.wait_ge(pre_copied, 2)
            pe.wait_ge(amb_ready, 1)

            with pe.Fori(0, B) as b:
                def open_misc(name):
                    s = SLOT[name]
                    pe.wait_ge(misc_drained[s % 2], b * (NM // 2) + s // 2)
                    return misc[s % 2]

                def open_sc(u):
                    pe.wait_ge(sc_drained[u % 2], b * (NSC // 2) + u // 2)
                    return sc[u % 2]

                def open_acc(u):
                    pe.wait_ge(acc_drained[u % 2], b * (N_ACC // 2) + u // 2)
                    return acc[u % 2]

                pe.wait_ge(xh_loaded, 16 * (b + 1))
                m = open_misc("xT")
                for n in range(N):
                    ins = nc.tensor.transpose(m[:, n * C:(n + 1) * C], xh[:, n, :], ident[:, :])
                ins.then_inc(misc_full, 1)
                wait_misc_drained(pe, b, "xT")
                for i in range(4):
                    m = open_misc(f"p{i}")
                    nc.tensor.matmul(m[:, :], w_cols[:, i, :], xT[:, :], start=True, stop=True).then_inc(misc_full, 1)
                for n in range(N):
                    m = open_misc(f"n{n}")
                    nc.tensor.matmul(m[:, 0:3 * P], xT[:, n * C:(n + 1) * C], w_nat[:, :], start=True, stop=True)\
                        .then_inc(misc_full, 1)

                pe.wait_ge(stacked[QA], 16 * NPROD * (b + 1))
                pe.wait_ge(stacked[KA], 16 * NPROD * (b + 1))
                q, k = stack[QA], stack[KA]
                for i, (mc, h0, nh) in enumerate(SOFT):
                    t = open_sc(SC_MAX + i)
                    w = 1024 // nh
                    mask = mask_first[:, :, :] if mc == 0 else mask_win[:, :, :, :]
                    for bank in range(2):
                        ins = nc.tensor.matmul(t[:, bank * 512:(bank + 1) * 512], ident16[:, :], mask,
                                               start=True, stop=False, skip_group_check=True)
                        if i == 0 and bank == 0:
                            ins.then_inc(xh_read, 1)
                        for hh in range(nh // 2):
                            hl = bank * nh // 2 + hh
                            ins = nc.tensor.matmul(t[:, hl * w:(hl + 1) * w],
                                                   q[0:KROWS, h0 + hl, mc * C:(mc + 1) * C],
                                                   k[0:KROWS, h0 + hl, (mc + 1) * C - w:(mc + 1) * C],
                                                   start=False, stop=True, skip_group_check=True)
                    ins.then_inc(sc_full, 1)

                def lin_scores(n):
                    for kk in range(2):
                        t = open_sc(SC_LIN + 2 * n + kk)
                        for hh in range(8):
                            ins = nc.tensor.matmul(t[:, hh * C:(hh + 1) * C],
                                                   stack[KS][0:KROWS, 8 * kk + hh, n * C:(n + 1) * C],
                                                   stack[QS][0:KROWS, 8 * kk + hh, n * C:(n + 1) * C],
                                                   start=True, stop=True)
                        ins.then_inc(sc_full, 1)

                pe.wait_ge(stacked[QS], 16 * NPROD * (b + 1))
                pe.wait_ge(stacked[KS], 16 * NPROD * (b + 1))
                lin_scores(0)
                lin_scores(1)
                pe.wait_ge(phi_ready, 3 * (b + 1))
                for n in range(N - 1):
                    m = open_misc(f"kv{n}")
                    nc.tensor.matmul(m[:, 0:H * (E + 1)], phi[:, 2, n * C:(n + 1) * C], v_s[:, n, :, 0:E + 1],
                                     start=True, stop=True).then_inc(misc_full, 1)
                wait_sc_drained(pe, b, SC_MAX + NT - 2)
                wait_sc_drained(pe, b, SC_MAX + NT - 1)
                m = open_misc("cT")
                for n in range(N):
                    ins = nc.tensor.transpose(m[0:H, n * C:(n + 1) * C], negc[:, n, :], ident[:, :])
                ins.then_inc(misc_full, 1)

                def to_tokens(u):
                    name = f"{'ls'[u // N]}{u % N}nat"
                    m = open_misc(name)
                    pe.wait_ge(acc_drained[u % 2], b * (N_ACC // 2) + u // 2 + 1)
                    for g in range(4):
                        ins = nc.tensor.transpose(m[:, g * C:(g + 1) * C], acc_s[u % 2][:, g * C:(g + 1) * C],
                                                  ident[:, :])
                    ins.then_inc(misc_full, 1)

                def to_columns(u):
                    name = f"{'ls'[u // N]}{u % N}T"
                    m = open_misc(name)
                    wait_misc_drained(pe, b, f"{'ls'[u // N]}{u % N}nat")
                    nc.tensor.transpose(m[:, 0:C], nat[u % 2][:, :], ident[:, :]).then_inc(misc_full, 1)

                def lin_out(n):
                    a = open_acc(n)
                    for g in range(4):
                        cols_g = slice(g * C, (g + 1) * C)
                        if n:
                            if n == 1:
                                wait_misc_drained(pe, b, "kv0")
                            else:
                                pe.wait_ge(state_ready, 2 * b + n - 1)
                            nc.tensor.matmul(a[:, cols_g], state[n - 1][:, 4 * g:4 * g + 4, :],
                                             phi[:, 0, n * C:(n + 1) * C], start=(g == 0), stop=False,
                                             skip_group_check=True)
                        t = 2 * n + g // 2
                        if g % 2 == 0:
                            wait_sc_drained(pe, b, SC_LIN + t)
                        for j in range(4):
                            ins = nc.tensor.matmul(a[32 * j:32 * j + VW, cols_g], v_s[:, n, 4 * g + j, :],
                                                   pa[t % PA][:, (4 * (g % 2) + j) * C:(4 * (g % 2) + j + 1) * C],
                                                   start=(n == 0 and g == 0), stop=True, skip_group_check=True)
                    ins.then_inc(acc_full, 1)

                for n in range(N):
                    lin_out(n)
                    if n + 2 < N:
                        lin_scores(n + 2)
                    if n >= 1:
                        to_tokens(n - 1)
                    if n >= 2:
                        to_columns(n - 2)
                to_tokens(N - 1)
                to_columns(N - 2)

                pe.wait_ge(c_stacked, 16 * CROWS * (b + 1))
                for i in range(NT + LAG + 8):
                    if i < NT:
                        mc, h0, nh = SOFT[i]
                        t = open_sc(SC_EXP + i)
                        half = 8 // nh
                        for hh in range(nh):
                            for w in range(half):
                                key = (mc - half + 1 + w) * C
                                o = (hh * half + w) * C
                                ins = nc.tensor.matmul(t[:, o:o + C], k[0:KROWS + CROWS, h0 + hh, key:key + C],
                                                       q[0:KROWS + CROWS, h0 + hh, mc * C:(mc + 1) * C],
                                                       start=True, stop=True)
                        ins.then_inc(sc_full, 1)
                    if i == 0:
                        to_columns(N - 1)
                    if LAG <= i < NT + LAG:
                        mc, h0, nh = SOFT[i - LAG]
                        first = h0 == 0
                        if first:
                            a = open_acc(N + mc)
                        pe.wait_ge(masked, b * NT + i - LAG + 1)
                        half = 8 // nh
                        p = pa[(N_LIN + i - LAG) % PA]
                        for g in range(nh // 4):
                            for w in range(half):
                                for j in range(4):
                                    hh = 4 * g + j
                                    o = (hh * half + w) * C
                                    gg = (h0 + hh) // 4
                                    ins = nc.tensor.matmul(
                                        a[32 * j:32 * j + VW, gg * C:(gg + 1) * C],
                                        v_a[:, mc - half + 1 + w, h0 + hh, :], p[:, o:o + C],
                                        start=(gg == 0 and w == 0), stop=(w == half - 1), skip_group_check=True)
                        ins.then_inc(pa_used, 1)
                    for mc in range(N):
                        if i == LAST_TILE[mc] + LAG + 2:
                            to_tokens(N + mc)
                        if i == LAST_TILE[mc] + LAG + 4:
                            to_columns(N + mc)
                m = open_misc("mix")
                for n in range(N):
                    pe_cols = slice(n * C, (n + 1) * C)
                    wait_misc_drained(pe, b, f"l{n}T")
                    wait_misc_drained(pe, b, f"s{n}T")
                    nc.tensor.matmul(m[:, pe_cols], oT[:, 0, pe_cols], w_mix[:, 1, :], start=True, stop=False)
                    ins = nc.tensor.matmul(m[:, pe_cols], oT[:, 1, pe_cols], w_mix[:, 0, :], start=False, stop=True)
                ins.then_inc(misc_full, 1)

            for t in range(B + 1):
                if t >= 2:
                    pe.wait_ge(pre_copied, 2 + t - 1)
                turned = sc[t % 2][:, 0:256].bitcast(BF16)
                if t < B:
                    for n in range(N):
                        ins = nc.tensor.transpose(turned[:, n * C:(n + 1) * C], xq[:, t, n * C:(n + 1) * C],
                                                  ident16[:, :])
                else:
                    ins = nc.tensor.transpose(turned[:, 0:P], wq[:, :], ident16[:, :])
                ins.then_inc(pre_full, 1)
            pe.wait_ge(pre_copied, 2 + B + 1)
            with pe.Fori(0, B) as b:
                m0 = NM * B
                d0 = B * (NM // 2) + 3 * b
                pe.wait_ge(h_ready, b + 1)
                pe.wait_ge(misc_drained[0], d0)
                for n in range(N):
                    ins = nc.tensor.transpose(misc[0][:, n * C:(n + 1) * C], hn[:, n, :], ident[:, :])
                ins.then_inc(misc_full, 1)
                pe.wait_ge(misc_drained[0], d0 + 1)
                for k in range(FC):
                    pe.wait_ge(misc_drained[(k + 1) % 2], d0 + (k + 1) // 2)
                    nc.tensor.matmul(misc[(k + 1) % 2][:, :], w1[:, k * P:(k + 1) * P], hT[:, :],
                                     start=True, stop=True).then_inc(misc_full, 1)
                pe.wait_ge(misc_drained[1], d0 + 2)
                for n in range(N):
                    ins = nc.tensor.matmul(misc[1][:, n * C:(n + 1) * C], xqT_all[:, bass.ds(b * L + n * C, C)],
                                           wqT[:, :], start=True, stop=True)
                ins.then_inc(misc_full, 1)
                pe.wait_ge(misc_drained[0], d0 + 3)
                pe.wait_ge(t2_ready, b)
                for n in range(N):
                    for k in range(FC):
                        ins = nc.tensor.matmul(sc[0][:, n * C:(n + 1) * C], hid[:, k, n * C:(n + 1) * C],
                                               w2[:, k, :], start=(k == 0), stop=(k == FC - 1))
                ins.then_inc(sc_full, 1)


_INS = ["x", "g1", "b1", "Wqkv_a", "bqkv_a", "Wp_a", "bp_a", "Wqkv_s", "bqkv_s", "Wo_s", "bo_s", "Wo", "bo",
        "gm", "bm", "W1", "b1m", "W2", "b2m"]
_INS = ["L0_attn_" + n for n in _INS] + ["L0_ffn_weight", "L0_ffn_bias"]


def kernel(**inputs):
    import numpy as _np
    import concourse.bacc as _bacc
    from concourse.bass_utils import run_bass_kernel_spmd as _run

    nc = _bacc.Bacc("TRN2", target_bir_lowering=False, num_devices=1)
    arrays, args = {}, []
    for name in _INS:
        a = _np.ascontiguousarray(inputs[name])
        arrays[name] = a
        args.append(nc.dram_tensor(name, a.shape, F32, kind="ExternalInput").ap())
    shape = arrays["L0_attn_x"].shape
    args.append(nc.dram_tensor("out", shape, F32, kind="ExternalOutput").ap())
    attention_block_kernel(nc, *args)
    r = _run(nc, [arrays], core_ids=[0])
    return r.results[0]["out"]
```

```python
from contextlib import ExitStack

import concourse.bass as bass
from concourse import mybir

P = 128
H = 16
E = 8
C = 128
VW = 32
NPROD = 6
KROWS = NPROD * E
CROWS = 3
KPAD = 96
NEG = -1e30
LN_EPS = 1e-5
DEN_EPS = 1e-6
ELU_SHIFT = 1e-4
FP8_MAX = 448.0
AMAX_MIN = 1e-12
FP8_MIN_NORMAL = 2.0 ** -6
FP8_ROUND = 1.5 * 2.0 ** 20
EXPONENT_BITS = 0x7F800000

ALU = mybir.AluOpType
ACT = mybir.ActivationFunctionType
BF16 = mybir.dt.bfloat16
F32 = mybir.dt.float32
I32 = mybir.dt.int32
U32 = mybir.dt.uint32
AX_X = mybir.AxisListType.X

QA, KA, QS, KS = range(4)


def attention_block_kernel(nc, x, g1, b1, Wqkv_a, bqkv_a, Wp_a, bp_a, Wqkv_s, bqkv_s, Wo_s, bo_s,
                           Wo, bo, gm, bm, W1, b1m, W2, b2m, ffn_w, ffn_b, out):
    B, L, D = x.shape
    N = L // C
    F = W1.shape[1]
    FC = F // P
    SCALE = float(E) ** -0.5
    assert D == P and H * E == D and B % 2 == 0

    Q_PARTS = [0, 0, 0, 1, 1, 2]
    K_PARTS = [0, 1, 2, 0, 1, 0]
    PARTS = {QA: Q_PARTS, KA: K_PARTS, QS: Q_PARTS, KS: K_PARTS}

    SOFT = [(0, 0, 8), (0, 8, 8)] + [(m, 4 * g, 4) for m in range(1, N) for g in range(4)]
    NT = len(SOFT)
    LAST_TILE = {m: max(i for i, t in enumerate(SOFT) if t[0] == m) for m in range(N)}

    PREP = ["xTa", "xTb", f"p{KS}", f"p{QS}", "vs", "kn", f"p{QA}", f"p{KA}"]
    LINEAR = ["l0nat", "l1nat", "l0T", "l2nat", "l1T", "l3nat", "l2T", "l3T", "cT"]
    MISC = {
        "start": PREP + ["va", "kv0", "kv1", "kv2"],
        "loop": LINEAR + PREP + ["s0nat", "s0T", "s1nat", "s1T", "s2nat", "s2T", "va", "s3nat", "kv0", "kv1",
                                 "s3T", "kv2", "mix"],
        "end": LINEAR + ["am", "s0nat", "s0T", "amb", "s1nat", "s1T", "s2nat", "s2T", "s3nat", "s3T", "mix"],
    }
    SLOT = {stage: {name: i for i, name in enumerate(names)} for stage, names in MISC.items()}
    M_START, M_LOOP, M_END = len(MISC["start"]), len(MISC["loop"]), len(MISC["end"])
    M_ALL = M_START + (B - 1) * M_LOOP + M_END
    assert M_START % 2 == M_LOOP % 2 == M_END % 2 == 0
    PA = 4
    N_LIN = 2 * N
    SC_ORDER = [("lin", i) for i in range(PA)]
    for i in range(NT):
        SC_ORDER += [("max", i)] + ([("lin", PA + i)] if PA + i < N_LIN else [])
    SC_ORDER += [("exp", i) for i in range(NT)]
    SC_SLOT = {use: i for i, use in enumerate(SC_ORDER)}
    NSC = len(SC_ORDER)
    assert NSC % 2 == 0
    N_ACC = 2 * N
    LAG = 3

    with ExitStack() as ctx:
        def sb(name, shape, dt=F32):
            return ctx.enter_context(nc.sbuf_tensor(name, shape, dt))

        def sem(name):
            return ctx.enter_context(nc.semaphore(name))

        ident = sb("ident", [P, P])
        ident16 = sb("ident16", [P, P], BF16)
        mask_win = sb("mask_win", [P, 2, 2, C], BF16)
        mask_first = sb("mask_first", [P, 4, C], BF16)
        own_head = sb("own_head", [P, H, E + 1])
        ones = sb("ones", [P, P])
        w_cols = sb("w_cols", [P, 4, P])
        w_nat = sb("w_nat", [P, 3 * P])
        wo = sb("wo", [P, P])
        w_mix = sb("w_mix", [P, 2, P])
        w1 = sb("w1", [P, F])
        w2 = sb("w2", [P, FC, P])
        wf = sb("wf", [P, P])
        wqT = sb("wqT", [P, P], BF16)
        cols = sb("cols", [P, 10])
        gb = sb("gb", [P, 4])
        b1c = sb("b1c", [P, FC])
        b_nat = sb("b_nat", [P, 3 * P])
        b_out = sb("b_out", [P, P])
        b_mix = sb("b_mix", [P, P])
        xn_all = sb("xn_all", [P, B, N, P])
        xh_all = sb("xh_all", [P, B, N, P])
        xq = sb("xq", [P, B, L], BF16)
        wq = sb("wq", [P, P], BF16)
        st_all = sb("st_all", [P, B, N, 6])
        xqT_all = sb("xqT_all", [P, B * N * P], BF16)
        mv = sb("mv", [P, B * N, 2])
        var = sb("var", [P, B * N])
        sd = sb("sd", [P, B * N])
        rs = sb("rs", [P, B * N])
        rt = sb("rt", [P, B * N])
        shift = sb("shift", [P, B * N])
        pre_col = sb("pre_col", [P, 1])
        am = sb("am", [P, 2])
        am1 = sb("am1", [1, 2])
        amb = sb("amb", [P, 2])
        fscale = sb("fscale", [P, 2])
        finv = sb("finv", [P, 2])
        dequant = sb("dequant", [P, 1])
        xh = sb("xh", [P, N, P])
        xT = sb("xT", [P, L])
        f = sb("f", [P, 4, L])
        parts = [sb(f"parts{i}", [P, 3, L], BF16) for i in range(4)]
        rest = sb("rest", [P, 4, L])
        stack = [sb(f"stack{i}", [P, H, L], BF16) for i in range(4)]
        v_a = sb("v_a", [P, N, H, VW])
        v_s = sb("v_s", [P, N, H, VW])
        k_lin = sb("k_lin", [P, L])
        phi = sb("phi", [P, 3, L])
        negc = sb("negc", [P, N, H])
        c_f = sb("c_f", [H, L])
        c_parts = sb("c_parts", [H, 3, L], BF16)
        kv_new = sb("kv_new", [P, H, E + 1])
        state = [sb(f"state{n}", [P, H, VW]) for n in range(1, N)]
        pa_all = sb("pa_all", [P, PA, 2 * 512])
        pa = [pa_all[:, i, :] for i in range(PA)]
        acc_s = [sb(f"acc_s{i}", [P, 512]) for i in range(2)]
        den = sb("den", [P, H])
        rden = sb("rden", [P, H])
        nat = [sb(f"nat{i}", [P, P]) for i in range(2)]
        oT = sb("oT", [P, 2, L])
        x1_all = xh_all
        c_rest = rest[0:H, 0, :]
        wp = pa_all[:, 2, 0:2 * P].rearrange("p (a d) -> p a d", a=2)
        wpT = pa_all[:, 2, 2 * P:4 * P].rearrange("p (a d) -> p a d", a=2)
        b_out2 = acc_s[0][:, 0:2 * P].rearrange("p (a d) -> p a d", a=2)
        bo_rows = acc_s[0][:, 2 * P:3 * P]
        pre = acc_s[1][:, 0:P]
        hn = xh
        hT = xT
        hid = f
        r1 = phi[:, 0, :]
        r2 = phi[:, 1, :]
        r3 = phi[:, 2, :]
        o_sb = k_lin
        q_e = rest

        sc = [ctx.enter_context(nc.psum_tensor(f"sc{i}", [P, 1024], F32)) for i in range(2)]
        acc = [ctx.enter_context(nc.psum_tensor(f"acc{i}", [P, 512], F32)) for i in range(2)]
        misc = [ctx.enter_context(nc.psum_tensor(f"misc{i}", [P, 512], F32)) for i in range(2)]

        x_loaded = [sem(f"x_loaded{b}") for b in range(B)]
        early_loaded = sem("early_loaded")
        late_loaded = sem("late_loaded")
        const_set = sem("const_set")
        ident_ready = sem("ident_ready")
        const_ready = sem("const_ready")
        stacks_cleared = sem("stacks_cleared")
        dve_step = sem("dve_step")
        var_ready = sem("var_ready")
        sd_ready = sem("sd_ready")
        shift_ready = sem("shift_ready")
        xh_ready = sem("xh_ready")
        bias_ready = sem("bias_ready")
        pre_ready = sem("pre_ready")
        pre_full = sem("pre_full")
        amax_ready = sem("amax_ready")
        quantised = sem("quantised")
        xh_loaded = sem("xh_loaded")
        misc_full = sem("misc_full")
        sc_full = sem("sc_full")
        acc_full = sem("acc_full")
        c_ready = sem("c_ready")
        c_stacked = sem("c_stacked")
        min_ready = sem("min_ready")
        exp_ready = sem("exp_ready")
        phi_ready = sem("phi_ready")
        state_ready = sem("state_ready")
        pa_used = sem("pa_used")
        tiles_taken = sem("tiles_taken")
        loads_begun = sem("loads_begun")
        lin_masked = sem("lin_masked")
        masked = sem("masked")
        h_ready = sem("h_ready")
        resid_ready = sem("resid_ready")
        out_ready = sem("out_ready")
        x_again = sem("x_again")
        stored = sem("stored")
        misc_drained = [sem("misc_drained0"), sem("misc_drained1")]
        sc_drained = [sem("sc_drained0"), sem("sc_drained1")]
        acc_drained = [sem("acc_drained0"), sem("acc_drained1")]
        parts_ready = [sem(f"parts_ready{i}") for i in range(4)]
        scratch_written = [sem(f"scratch_written{i}") for i in range(4)]
        stacked = [sem(f"stacked{i}") for i in range(4)]
        scratch = [nc.dram_tensor(f"scratch{i}", (P, 3, L), BF16, kind="Internal").ap() for i in range(4)]
        x_dram = x.rearrange("b (n p) d -> b p n d", p=P)
        out_dram = out.rearrange("b (n p) d -> b p n d", p=P)

        early_cols = [
            (cols[:, 4:5], g1), (cols[:, 5:6], b1), (cols[:, 0:2], bqkv_a[0:2 * P]), (cols[:, 2:4], bqkv_s[0:2 * P]),
        ]
        early = [
            (w_cols[:, KS, :], Wqkv_s[:, P:2 * P]), (w_cols[:, QS, :], Wqkv_s[:, 0:P]),
            (w_nat[:, P:2 * P], Wqkv_s[:, 2 * P:3 * P]), (w_nat[:, 2 * P:3 * P], Wqkv_s[:, P:2 * P]),
            (w_cols[:, QA, :], Wqkv_a[:, 0:P]), (w_cols[:, KA, :], Wqkv_a[:, P:2 * P]),
            (w_nat[:, 0:P], Wqkv_a[:, 2 * P:3 * P]),
            (b_nat[:, P:2 * P], bqkv_s[2 * P:3 * P].partition_broadcast(P)),
            (b_nat[:, 2 * P:3 * P], bqkv_s[P:2 * P].partition_broadcast(P)),
            (b_nat[:, 0:P], bqkv_a[2 * P:3 * P].partition_broadcast(P)),
        ]
        late = [
            (wp[:, 0, :], Wp_a), (wp[:, 1, :], Wo_s), (wo[:, :], Wo),
            (bo_rows, bo.partition_broadcast(P)),
            (b_out2[:, 0, :], b2m.partition_broadcast(P)), (b_out2[:, 1, :], ffn_b.partition_broadcast(P)),
            (w1[:, :], W1), (w2[:, :, :], W2.rearrange("(k p) d -> p k d", p=P)), (wf[:, :], ffn_w),
        ]
        late_cols = [(cols[:, 6:7], gm), (cols[:, 7:8], bm), (cols[:, 8:9], bp_a), (cols[:, 9:10], bo_s),
                  (b1c[:, :], b1m)]
        EARLY_ALL = 16 * (len(early) + len(early_cols))
        LATE_ALL = 16 * (len(late) + len(late_cols))
        CONST_ALL = 9
        PRE_FULL = 4
        SC_MLP = 1 + B * (NSC // 2) + 3

        class Use:

            def __init__(self, stage, b, name):
                slot = SLOT[stage][name]
                before = {"start": 0, "loop": M_START, "end": M_START + (B - 1) * M_LOOP}[stage]
                self.parity = slot % 2
                self.bank = misc[slot % 2]
                self.drained = misc_drained[slot % 2]
                if stage == "loop":
                    self.count_full = b * M_LOOP + (before + slot + 1)
                    self.count_open = b * (M_LOOP // 2) + (before // 2 + slot // 2)
                else:
                    self.count_full = before + slot + 1
                    self.count_open = before // 2 + slot // 2
                self.count_drained = self.count_open + 1

        def wait_misc_full(eng, it, name):
            eng.wait_ge(misc_full, Use(*it, name).count_full)

        def wait_misc_drained(eng, it, name):
            use = Use(*it, name)
            eng.wait_ge(use.drained, use.count_drained)

        def sc_of(use):
            return sc[SC_SLOT[use] % 2]

        def wait_sc_full(eng, b, use):
            eng.wait_ge(sc_full, b * NSC + SC_SLOT[use] + 1)

        def wait_sc_drained(eng, b, use):
            u = SC_SLOT[use]
            eng.wait_ge(sc_drained[u % 2], b * (NSC // 2) + u // 2 + 2)

        def unit(u):
            return f"{'ls'[u // N]}{u % N}"

        def apart(eng):
            eng.wait_ge(const_ready, 1)

        block = ctx.enter_context(nc.Block())

        @block.sync
        def _(sp):
            sp.dma_start(xn_all[:, 0, :, :], x_dram[0]).then_inc(x_loaded[0], 16)
            for dst, src in early:
                sp.dma_start(dst, src).then_inc(early_loaded, 16)
            for b in range(1, B):
                sp.dma_start(xn_all[:, b, :, :], x_dram[b]).then_inc(x_loaded[b], 16)
            for dst, src in late:
                sp.dma_start(dst, src).then_inc(late_loaded, 16)
            for dst, src in late_cols:
                sp.dma_start(dst, src.rearrange("(k p) -> p k", p=P), allow_slow_non_contiguous=True)\
                  .then_inc(late_loaded, 16)

            def load_tokens(b):
                apart(sp)
                sp.wait_ge(xh_ready, b + 1)
                sp.dma_start(xh[:, :, :], xh_all[:, b, :, :]).then_inc(xh_loaded, 16)

            def write_parts(i, b, first=False):
                apart(sp)
                sp.wait_ge(parts_ready[i], b + 1)
                if not first:
                    apart(sp)
                    sp.wait_ge(stacked[i], 16 * NPROD * b)
                sp.dma_start(scratch[i], parts[i][:, :, :]).then_inc(scratch_written[i], 16)

            def load_stack(i, b):
                apart(sp)
                sp.wait_ge(scratch_written[i], 16 * (b + 1))
                for g, part in enumerate(PARTS[i]):
                    sp.dma_start(stack[i][g * E:(g + 1) * E, :, :],
                                 scratch[i][:, part, :].rearrange("(h e) t -> e h t", e=E))\
                      .then_inc(stacked[i], 16)

            def load_maxima(b):
                apart(sp)
                sp.wait_ge(c_ready, b + 1)
                for r in range(CROWS):
                    sp.dma_start(stack[QA][KPAD + r:KPAD + r + 1, :, :], c_parts[:, r, :]).then_inc(c_stacked, 16)

            load_tokens(0)
            sp.wait_ge(stacks_cleared, 5)
            for pair in ((KS, QS), (QA, KA)):
                for i in pair:
                    write_parts(i, 0, first=True)
                for i in pair:
                    load_stack(i, 0)
            with sp.Fori(0, B - 1) as b:
                load_tokens(b + 1)
                load_maxima(b)
                for i in (KS, QS):
                    write_parts(i, b + 1)
                apart(sp)
                wait_sc_full(sp, b, ("lin", N_LIN - 1))
                sp.sem_inc(loads_begun, 1)
                for i in (KS, QS):
                    load_stack(i, b + 1)
                for i in (QA, KA):
                    write_parts(i, b + 1)
                apart(sp)
                wait_sc_full(sp, b, ("exp", NT - 1))
                sp.sem_inc(loads_begun, 1)
                for i in (QA, KA):
                    load_stack(i, b + 1)
            load_maxima(B - 1)
            sp.wait_ge(misc_full, M_ALL)
            r3_rows = r3.rearrange("p (n d) -> p n d", d=P)
            sp.dma_start(r3_rows, x_dram[0]).then_inc(x_again, 16)
            with sp.Fori(0, B - 1) as b:
                apart(sp)
                sp.wait_ge(out_ready, b + 1)
                sp.dma_start(out_dram[b], o_sb[:, :].rearrange("p (n d) -> p n d", d=P)).then_inc(stored, 16)
                apart(sp)
                sp.wait_ge(stored, 16 * b + 16)
                sp.dma_start(r3_rows, x_dram[b + 1]).then_inc(x_again, 16)
            sp.wait_ge(out_ready, B)
            sp.dma_start(out_dram[B - 1], o_sb[:, :].rearrange("p (n d) -> p n d", d=P)).then_inc(stored, 16)
            sp.wait_ge(stored, 16 * B)

        @block.gpsimd
        def _(pool):
            for tile, value in ((ident, 0.0), (v_s, 1.0)):
                pool.memset(tile[tuple(slice(None) for _ in tile.shape)], value).then_inc(const_set, 1)
            pool.wait_ge(const_set, 2)
            pool.affine_select(out=ident[:, :], in_=ident[:, :], pattern=[[-1, P]], compare_op=ALU.not_equal,
                               fill=1.0, base=0, channel_multiplier=1).then_inc(ident_ready, 1)
            for i in (KS, QS, QA, KA):
                pool.memset(stack[i][:, :, :].rearrange("p h t -> p (h t)").bitcast(U32), 0)\
                    .then_inc(stacks_cleared, 1)
            for tile, value in ((ident16, 0.0), (mask_win, 0.0), (mask_first, 0.0), (own_head, 1.0), (v_a, 1.0),
                                (ones, 1.0)):
                pool.memset(tile[tuple(slice(None) for _ in tile.shape)], value).then_inc(const_set, 1)
            for s in state:
                pool.memset(s[:, :, :], 0.0).then_inc(const_set, 1)
            pool.wait_ge(stacks_cleared, 4)
            pool.wait_ge(const_set, 8 + len(state))
            pool.memset(stack[KA][KPAD:P, :, :].rearrange("p h t -> p (h t)").bitcast(U32), 0x3F803F80)\
                .then_inc(stacks_cleared, 1)
            pool.wait_ge(stacks_cleared, 5)
            pool.affine_select(out=ident16[:, :], in_=ident16[:, :], pattern=[[-1, P]], compare_op=ALU.not_equal,
                               fill=1.0, base=0, channel_multiplier=1).then_inc(const_ready, 1)
            pool.affine_select(out=mask_win[:, :, 0, :], in_=mask_win[:, :, 0, :], pattern=[[0, 2], [1, C]],
                               compare_op=ALU.is_gt, fill=NEG, base=0, channel_multiplier=-1)\
                .then_inc(const_ready, 1)
            pool.affine_select(out=mask_win[:, :, 1, :], in_=mask_win[:, :, 1, :], pattern=[[0, 2], [-1, C]],
                               compare_op=ALU.is_ge, fill=NEG, base=0, channel_multiplier=1)\
                .then_inc(const_ready, 1)
            pool.affine_select(out=mask_first[:, :, :], in_=mask_first[:, :, :], pattern=[[0, 4], [-1, C]],
                               compare_op=ALU.is_ge, fill=NEG, base=0, channel_multiplier=1)\
                .then_inc(const_ready, 1)
            pool.affine_select(out=own_head[:, :, :], in_=own_head[:, :, :], pattern=[[-E, H], [0, E + 1]],
                               compare_op=ALU.is_ge, fill=0.0, base=0, channel_multiplier=1)\
                .then_inc(const_ready, 1)
            pool.wait_ge(const_ready, 5)
            pool.affine_select(out=own_head[:, :, :], in_=own_head[:, :, :], pattern=[[E, H], [0, E + 1]],
                               compare_op=ALU.is_ge, fill=0.0, base=E - 1, channel_multiplier=-1)\
                .then_inc(const_ready, 1)
            for v in (v_a, v_s):
                pool.memset(v[:, :, :, E + 1:VW], 0.0).then_inc(const_ready, 1)
            pool.wait_ge(const_ready, 8)
            pool.wait_ge(late_loaded, LATE_ALL)
            pool.tensor_tensor(b_out[:, :], b_out2[:, 0, :], b_out2[:, 1, :], ALU.add).then_inc(const_ready, 1)

            def masks(b):
                for t in range(N_LIN):
                    wait_sc_drained(pool, b, ("lin", t))
                    pool.sem_inc(tiles_taken, 1)
                    p = pa[t % PA].rearrange("p (h r) -> p h r", r=C)
                    pool.affine_select(out=p, in_=p, pattern=[[0, 8], [1, C]], compare_op=ALU.is_ge,
                                       fill=0.0, base=0, channel_multiplier=-1).then_inc(lin_masked, 1)
                for i, (m, h0, nh) in enumerate(SOFT):
                    wait_sc_drained(pool, b, ("exp", i))
                    pool.sem_inc(tiles_taken, 1)
                    k = (N_LIN + i) % PA
                    if m == 0:
                        p = pa[k].rearrange("p (h r) -> p h r", r=C)
                        pool.affine_select(out=p, in_=p, pattern=[[0, nh], [1, C]], compare_op=ALU.is_ge,
                                           fill=0.0, base=0, channel_multiplier=-1).then_inc(masked, 1)
                    else:
                        p = pa[k].rearrange("p (h w r) -> p h w r", w=2, r=C)
                        pool.affine_select(out=p[:, :, 0, :], in_=p[:, :, 0, :], pattern=[[0, nh], [-1, C]],
                                           compare_op=ALU.is_gt, fill=0.0, base=0, channel_multiplier=1)
                        pool.affine_select(out=p[:, :, 1, :], in_=p[:, :, 1, :], pattern=[[0, nh], [1, C]],
                                           compare_op=ALU.is_ge, fill=0.0, base=0, channel_multiplier=-1)\
                            .then_inc(masked, 1)

            with pool.Fori(0, B - 1) as b:
                masks(b)
            masks(B - 1)

            with pool.Fori(0, B) as b:
                pool.wait_ge(x_again, 16 * (b + 1))
                pool.tensor_tensor(r3.rearrange("p (n d) -> p n d", d=P), r3.rearrange("p (n d) -> p n d", d=P),
                                   b_out[:, :].rearrange("p (a d) -> p a d", a=1).to_broadcast([P, N, P]),
                                   ALU.add).then_inc(resid_ready, 1)
                pool.wait_ge(resid_ready, b + 1)
                pool.wait_ge(sc_drained[0], SC_MLP + b + 1)
                pool.tensor_tensor(o_sb[:, :], r2, r3, ALU.add).then_inc(out_ready, 1)

        @block.scalar
        def _(act):
            for dst, src in early_cols:
                act.dma_start(dst, src.rearrange("(k p) -> p k", p=P), allow_slow_non_contiguous=True)\
                   .then_inc(early_loaded, 16)

            def norms(j, first, last):
                tokens = slice(first * N, last * N)
                for k in range(2):
                    act.wait_ge(var_ready, 2 * j + k + 1)
                    nc.scalar.activation(sd[:, tokens], var[:, tokens], ACT.Sqrt).then_inc(sd_ready, 1)
                act.wait_ge(shift_ready, j + 1)
                for b in range(first, last):
                    for n in range(N):
                        t = b * N + n
                        ins = nc.scalar.activation(xh_all[:, b, n, :], xn_all[:, b, n, :], ACT.Identity,
                                                   scale=rs[:, t:t + 1], bias=shift[:, t:t + 1])
                    ins.then_inc(xh_ready, 1)

            def drain(it, name, dst, src, func=ACT.Copy, **kw):
                use = Use(*it, name)
                act.wait_ge(misc_full, use.count_full)
                nc.scalar.activation(dst, use.bank[src], func, **kw).then_inc(use.drained, 1)

            def prepare(it, b):
                everything = (slice(None), slice(None))
                half = L // 2
                for k, name in enumerate(("xTa", "xTb")):
                    drain(it, name, xT[:, k * half:(k + 1) * half], (slice(None), slice(0, half)), ACT.Identity,
                          scale=cols[:, 4:5], bias=cols[:, 5:6])

                def project(i):
                    if it[0] != "start":
                        act.wait_ge(parts_ready[i], b)
                    drain(it, f"p{i}", f[:, i, :], everything, ACT.Identity,
                          scale=SCALE if i in (QA, QS) else 1.0, bias=gb[:, i:i + 1])

                def exp_min(c):
                    j = (1, 0, 2)[c]
                    act.wait_ge(min_ready, 3 * b + c + 1)
                    nc.scalar.activation(phi[:, j, :], phi[:, j, :], ACT.Exp).then_inc(exp_ready, 1)

                project(KS)
                project(QS)
                exp_min(0)
                project(QA)
                exp_min(1)
                project(KA)
                exp_min(2)

            def copy_lin(b, t):
                wait_sc_full(act, b, ("lin", t))
                if t >= PA:
                    act.wait_ge(acc_full, b * N + (t - PA) // 2 + 1)
                nc.scalar.activation(pa[t % PA], sc_of(("lin", t))[:, :], ACT.Copy)\
                    .then_inc(sc_drained[SC_SLOT["lin", t] % 2], 1)

            def save_acc(it, b, u):
                if u < N:
                    act.wait_ge(acc_full, b * N + u + 1)
                else:
                    act.wait_ge(pa_used, b * NT + LAST_TILE[u - N] + 1)
                if u >= 2:
                    wait_misc_full(act, it, unit(u - 2) + "nat")
                nc.scalar.activation(acc_s[u % 2][:, :], acc[u % 2][:, :], ACT.Copy)\
                    .then_inc(acc_drained[u % 2], 1)

            def save_T(it, u):
                kind, n = u // N, u % N
                drain(it, unit(u) + "T", oT[:, kind, n * C:(n + 1) * C], (slice(None), slice(0, C)))

            def attend(it, b):
                for t in range(6):
                    copy_lin(b, t)
                save_acc(it, b, 0)
                copy_lin(b, 6)
                copy_lin(b, 7)
                save_acc(it, b, 1)
                save_acc(it, b, 2)
                save_T(it, 0)
                save_acc(it, b, 3)
                for n in range(1, N):
                    save_T(it, n)
                drain(it, "cT", c_f[:, :], (slice(0, H), slice(None)))
                if it[0] == "loop":
                    prepare(it, b + 1)
                for i in range(NT + 8):
                    if i < NT:
                        wait_sc_full(act, b, ("exp", i))
                        if i < PA:
                            act.wait_ge(acc_full, b * N + (N_LIN - PA + i) // 2 + 1)
                        else:
                            act.wait_ge(pa_used, b * NT + i - PA + 1)
                        nc.scalar.activation(pa[(N_LIN + i) % PA], sc_of(("exp", i))[:, :], ACT.Exp)\
                            .then_inc(sc_drained[SC_SLOT["exp", i] % 2], 1)
                    for m in range(N):
                        if i == LAST_TILE[m] + LAG + 1:
                            save_acc(it, b, N + m)
                        if i == LAST_TILE[m] + LAG + 5:
                            save_T(it, N + m)

            norms(0, 0, 1)
            act.wait_ge(early_loaded, EARLY_ALL)
            act.wait_ge(bias_ready, 2)
            prepare(("start", 0), 0)
            act.wait_ge(pre_full, 2)
            for k in range(2):
                nc.scalar.activation(wpT[:, k, :], sc[k][:, 0:P], ACT.Copy).then_inc(sc_drained[k], 1)
            act.wait_ge(pre_full, 3)
            nc.scalar.activation(w_mix[:, :, :], acc[0][:, 0:2 * P].rearrange("p (a d) -> p a d", a=2), ACT.Copy)\
                .then_inc(acc_drained[0], 1)
            norms(1, 1, B)

            with act.Fori(0, B - 1) as b:
                attend(("loop", b), b)
            attend(("end", B - 1), B - 1)

            act.wait_ge(var_ready, 5)
            nc.scalar.activation(sd[:, :], var[:, :], ACT.Sqrt).then_inc(sd_ready, 1)
            for t in range(B + 1):
                act.wait_ge(pre_full, PRE_FULL + t + 1)
                width = L if t < B else P
                dst = xqT_all[:, t * L:(t + 1) * L] if t < B else wqT[:, :]
                nc.scalar.activation(dst, sc[t % 2][:, 0:width // 2].bitcast(BF16), ACT.Copy)\
                    .then_inc(sc_drained[t % 2], 1)
            with act.Fori(0, B) as b:
                act.wait_ge(sc_full, NSC * B + b)
                for k in range(FC):
                    act.wait_ge(misc_full, M_ALL + 6 * b + 2 + k)
                    nc.scalar.activation(hid[:, k, :], misc[(1 + k) % 2][:, :], ACT.Gelu, bias=b1c[:, k:k + 1])\
                        .then_inc(misc_drained[(1 + k) % 2], 1)

        @block.vector
        def _(dve):
            done = [0]
            base = [0]

            def step(ins):
                done[0] += 1
                ins.then_inc(dve_step, 1)
                dve.wait_ge(dve_step, base[0] + done[0])

            def rsqrt(tokens, j):
                ve, root, r, t = var[:, tokens], sd[:, tokens], rs[:, tokens], rt[:, tokens]
                nc.vector.tensor_scalar(ve, mv[:, tokens, 1], LN_EPS, None, ALU.add).then_inc(var_ready, 1)
                dve.wait_ge(sd_ready, j)
                step(nc.vector.reciprocal(r, root))
                step(nc.vector.tensor_tensor(t, r, r, ALU.mult))
                step(nc.vector.tensor_tensor(t, t, ve, ALU.mult))
                step(nc.vector.tensor_scalar(t, t, -0.5, 1.5, ALU.mult, ALU.add))
                step(nc.vector.tensor_tensor(r, r, t, ALU.mult))

            def norms(j, first, last):
                tokens = slice(first * N, last * N)
                for k in range(2):
                    for t in range(first * N, last * N):
                        if k == 0 and t % N == 0:
                            dve.wait_ge(x_loaded[t // N], 16)
                        ins = nc.vector.bn_stats(st_all[:, t // N, t % N, :], xn_all[:, t // N, t % N, :])
                    step(ins)
                    for t in range(first * N, last * N):
                        ins = nc.vector.bn_aggr(mv[:, t, :], st_all[:, t // N, t % N, :])
                    step(ins)
                    rsqrt(tokens, 2 * j + k + 1)
                    if k == 0:
                        for t in range(first * N, last * N):
                            x_t = xn_all[:, t // N, t % N, :]
                            ins = nc.vector.tensor_scalar(x_t, x_t, mv[:, t, 0:1], rs[:, t:t + 1],
                                                          ALU.subtract, ALU.mult)
                        step(ins)
                    else:
                        nc.vector.scalar_tensor_tensor(out=shift[:, tokens], in0=mv[:, tokens, 0], scalar=-1.0,
                                                       in1=rs[:, tokens], op0=ALU.mult, op1=ALU.mult)\
                            .then_inc(shift_ready, 1)

            def add_rows(it, name, v, o):
                use = Use(*it, name)
                dve.wait_ge(misc_full, use.count_full)
                row = b_nat[:, o:o + P].rearrange("p (h e) -> p h e", e=E)
                for n in range(N):
                    ins = nc.vector.tensor_tensor(v[:, n, :, 0:E],
                                                  use.bank[:, n * C:(n + 1) * C].rearrange("p (h e) -> p h e", e=E),
                                                  row, ALU.add)
                ins.then_inc(use.drained, 1)

            def split(i, src):
                step(nc.vector.tensor_copy(parts[i][:, 0, :], src))
                step(nc.vector.tensor_tensor(rest[:, i, :], src, parts[i][:, 0, :], ALU.subtract))
                step(nc.vector.tensor_copy(parts[i][:, 1, :], rest[:, i, :]))
                nc.vector.tensor_tensor(parts[i][:, 2, :], rest[:, i, :], parts[i][:, 1, :], ALU.subtract)\
                    .then_inc(parts_ready[i], 1)

            def prepare_linear(it, b):
                for i, j in ((KS, 1), (QS, 0)):
                    wait_misc_drained(dve, it, f"p{i}")
                    nc.vector.tensor_scalar(phi[:, j, :], f[:, i, :], 0.0, None, ALU.min).then_inc(min_ready, 1)
                    step(nc.vector.tensor_scalar(f[:, i, :], f[:, i, :], 0.0, ELU_SHIFT, ALU.max, ALU.add))
                add_rows(it, "vs", v_s, P)
                use = Use(*it, "kn")
                dve.wait_ge(misc_full, use.count_full)
                nc.vector.tensor_tensor(k_lin[:, :].rearrange("p (n d) -> p n d", d=P),
                                        use.bank[:, :].rearrange("p (n d) -> p n d", d=P),
                                        b_nat[:, 2 * P:3 * P].rearrange("p (a d) -> p a d", a=1)
                                        .to_broadcast([P, N, P]), ALU.add).then_inc(use.drained, 1)
                dve.wait_ge(use.drained, use.count_drained)
                nc.vector.tensor_scalar(phi[:, 2, :], k_lin[:, :], 0.0, None, ALU.min).then_inc(min_ready, 1)
                step(nc.vector.tensor_scalar(k_lin[:, :], k_lin[:, :], 0.0, ELU_SHIFT, ALU.max, ALU.add))
                for c, (i, j) in enumerate(((KS, 1), (QS, 0))):
                    dve.wait_ge(exp_ready, 3 * b + c + 1)
                    nc.vector.tensor_tensor(phi[:, j, :], phi[:, j, :], f[:, i, :], ALU.add).then_inc(phi_ready, 1)
                    dve.wait_ge(phi_ready, 3 * b + c + 1)
                    split(i, phi[:, j, :])
                dve.wait_ge(exp_ready, 3 * b + 3)
                nc.vector.tensor_tensor(phi[:, 2, :], phi[:, 2, :], k_lin[:, :], ALU.add).then_inc(phi_ready, 1)

            def prepare_window(it, i):
                wait_misc_drained(dve, it, f"p{i}")
                split(i, f[:, i, :])

            def add_state(it, b, n):
                use = Use(*it, f"kv{n}")
                dve.wait_ge(misc_full, use.count_full)
                m = use.bank[:, 0:H * (E + 1)].rearrange("p (h f) -> p h f", h=H)
                if n == 0:
                    nc.vector.tensor_tensor(state[0][:, :, 0:E + 1], m, own_head[:, :, :], ALU.mult)\
                        .then_inc(use.drained, 1)
                else:
                    if n > 1:
                        dve.wait_ge(state_ready, 2 * b + n - 1)
                    nc.vector.tensor_tensor(kv_new[:, :, :], m, own_head[:, :, :], ALU.mult)\
                        .then_inc(use.drained, 1)
                    dve.wait_ge(use.drained, use.count_drained)
                    if n == 1:
                        wait_misc_drained(dve, it, "kv0")
                    nc.vector.tensor_tensor(state[n][:, :, 0:E + 1], state[n - 1][:, :, 0:E + 1],
                                            kv_new[:, :, :], ALU.add).then_inc(state_ready, 1)

            def top(b, i):
                m, h0, nh = SOFT[i]
                wait_sc_full(dve, b, ("max", i))
                nc.vector.tensor_reduce(negc[:, m, h0:h0 + nh],
                                        sc_of(("max", i))[:, :].rearrange("p (h s) -> p h s", h=nh),
                                        AX_X, ALU.max, negate=True).then_inc(sc_drained[SC_SLOT["max", i] % 2], 1)

            def normalise(it, u):
                kind = u // N
                use = Use(*it, unit(u) + "nat")
                dve.wait_ge(misc_full, use.count_full)
                m = use.bank[:, :].rearrange("p (h f) -> p h f", f=VW)
                step(nc.vector.tensor_scalar(den[:, :], m[:, :, E], 0.0 if kind else DEN_EPS, None, ALU.add))
                step(nc.vector.reciprocal(rden[:, :], den[:, :]))
                if u >= 2:
                    wait_misc_full(dve, it, unit(u - 2) + "T")
                nc.vector.tensor_tensor(nat[u % 2][:, :].rearrange("p (h e) -> p h e", e=E), m[:, :, 0:E],
                                        rden[:, :].rearrange("p (h a) -> p h a", a=1).to_broadcast([P, H, E]),
                                        ALU.mult).then_inc(use.drained, 1)

            y, big = q_e[:, QS, :], q_e[:, KS, :]

            def quantise(k, dst, src, scale, w):
                if k:
                    dve.wait_ge(quantised, k)
                step(nc.vector.tensor_scalar(y[:, 0:w], src, scale, None, ALU.mult))
                step(nc.vector.tensor_scalar(big[:, 0:w].bitcast(I32), y[:, 0:w].bitcast(I32),
                                             EXPONENT_BITS, None, ALU.bitwise_and))
                step(nc.vector.tensor_scalar(big[:, 0:w], big[:, 0:w], FP8_MIN_NORMAL, FP8_ROUND,
                                             ALU.max, ALU.mult))
                step(nc.vector.tensor_tensor(y[:, 0:w], y[:, 0:w], big[:, 0:w], ALU.add))
                nc.vector.tensor_tensor(dst, y[:, 0:w], big[:, 0:w], ALU.subtract).then_inc(quantised, 1)

            def attend(it, b):
                more = it[0] == "loop"
                after = {4: 0, 6: 1, 8: 2, 10: 3}
                for i in range(NT):
                    top(b, i)
                    if i in after:
                        normalise(it, after[i])
                wait_misc_drained(dve, it, "cT")
                step(nc.vector.tensor_copy(c_parts[:, 0, :], c_f[:, :]))
                step(nc.vector.tensor_tensor(c_rest, c_f[:, :], c_parts[:, 0, :], ALU.subtract))
                step(nc.vector.tensor_copy(c_parts[:, 1, :], c_rest))
                nc.vector.tensor_tensor(c_parts[:, 2, :], c_rest, c_parts[:, 1, :], ALU.subtract)\
                    .then_inc(c_ready, 1)
                if more:
                    prepare_linear(it, b + 1)
                    normalise(it, N)
                    prepare_window(it, QA)
                    normalise(it, N + 1)
                    prepare_window(it, KA)
                    normalise(it, N + 2)
                    add_rows(it, "va", v_a, 0)
                    normalise(it, N + 3)
                    for n in range(N - 1):
                        add_state(it, b + 1, n)
                else:
                    nc.vector.tensor_reduce(am[:, 0:1], xn_all[:, :, :, :].rearrange("p b n d -> p (b n d)"),
                                            AX_X, ALU.max, apply_absolute_value=True)
                    nc.vector.tensor_reduce(am[:, 1:2], wf[:, :], AX_X, ALU.max, apply_absolute_value=True)\
                        .then_inc(amax_ready, 1)
                    use = Use(*it, "am")
                    dve.wait_ge(misc_full, use.count_full)
                    nc.vector.tensor_reduce(am1[:, :], use.bank[0:1, 0:2 * P].rearrange("p (a d) -> p a d", a=2),
                                            AX_X, ALU.max).then_inc(use.drained, 1)
                    dve.wait_ge(use.drained, use.count_drained)
                    nc.vector.tensor_scalar(am1[:, :], am1[:, :], AMAX_MIN, None, ALU.max).then_inc(amax_ready, 1)
                    normalise(it, N)
                    use = Use(*it, "amb")
                    dve.wait_ge(misc_full, use.count_full)
                    nc.vector.tensor_copy(amb[:, :], use.bank[:, 0:2]).then_inc(use.drained, 1)
                    dve.wait_ge(use.drained, use.count_drained)
                    step(nc.vector.reciprocal(amb[:, :], amb[:, :]))
                    step(nc.vector.tensor_scalar(fscale[:, :], amb[:, :], FP8_MAX, None, ALU.mult))
                    step(nc.vector.reciprocal(finv[:, :], fscale[:, :]))
                    step(nc.vector.tensor_tensor(dequant[:, :], finv[:, 0:1], finv[:, 1:2], ALU.mult))
                    rows = [xn_all[:, t, :, :].rearrange("p n d -> p (n d)") for t in range(B)]
                    quantise(0, xq[:, 0, :], rows[0], fscale[:, 0:1], L)
                    normalise(it, N + 1)
                    quantise(1, xq[:, 1, :], rows[1], fscale[:, 0:1], L)
                    normalise(it, N + 2)
                    quantise(2, xq[:, 2, :], rows[2], fscale[:, 0:1], L)
                    quantise(3, xq[:, 3, :], rows[3], fscale[:, 0:1], L)
                    quantise(B, wq[:, :], wf[:, :], fscale[:, 1:2], P)
                    normalise(it, N + 3)
                use = Use(*it, "mix")
                dve.wait_ge(misc_full, use.count_full)
                step(nc.vector.tensor_tensor(x1_all[:, b, :, :], use.bank[:, :].rearrange("p (n d) -> p n d", d=P),
                                             xn_all[:, b, :, :], ALU.add))
                nc.vector.tensor_tensor(x1_all[:, b, :, :], x1_all[:, b, :, :],
                                        b_mix[:, :].rearrange("p (a d) -> p a d", a=1).to_broadcast([P, N, P]),
                                        ALU.add).then_inc(use.drained, 1)

            norms(0, 0, 1)
            dve.wait_ge(early_loaded, EARLY_ALL)
            nc.vector.tensor_scalar(gb[:, :], cols[:, 0:4], 1.0, None, ALU.mult).then_inc(bias_ready, 1)
            dve.wait_ge(bias_ready, 1)
            nc.vector.tensor_scalar(gb[:, 0:4:2], cols[:, 0:4:2], SCALE, None, ALU.mult).then_inc(bias_ready, 1)
            start = ("start", 0)
            dve.wait_ge(const_ready, CONST_ALL - 1)
            prepare_linear(start, 0)
            prepare_window(start, QA)
            prepare_window(start, KA)
            dve.wait_ge(late_loaded, LATE_ALL)
            step(nc.vector.tensor_scalar(pre_col[:, :], cols[:, 8:9], cols[:, 9:10], None, ALU.add))
            nc.vector.tensor_scalar(pre, ones[:, :], pre_col[:, :], None, ALU.mult).then_inc(pre_ready, 1)
            add_rows(start, "va", v_a, 0)
            for n in range(N - 1):
                add_state(start, 0, n)
            dve.wait_ge(pre_full, PRE_FULL)
            nc.vector.tensor_tensor(b_mix[:, :], acc[1][:, 0:P], bo_rows, ALU.add).then_inc(acc_drained[1], 1)
            norms(1, 1, B)
            before = done[0]
            LOOP_STEPS = 3 + 3 + 12 + 2 * N_ACC + 1
            done[0] = 0
            with dve.Fori(0, B - 1) as b:
                base[0] = b * LOOP_STEPS + before
                attend(("loop", b), b)
            assert done[0] == LOOP_STEPS
            base[0] = 0
            done[0] = before + (B - 1) * LOOP_STEPS
            attend(("end", B - 1), B - 1)

            wait_misc_drained(dve, ("end", B - 1), "mix")
            for t in range(B * N):
                ins = nc.vector.bn_stats(st_all[:, t // N, t % N, :], x1_all[:, t // N, t % N, :])
            step(ins)
            for t in range(B * N):
                ins = nc.vector.bn_aggr(mv[:, t, :], st_all[:, t // N, t % N, :])
            step(ins)
            rsqrt(slice(0, B * N), 5)

            def norm_tokens(b):
                for n in range(N):
                    ins = nc.vector.tensor_scalar(hn[:, n, :], x1_all[:, b, n, :], mv[:, b * N + n, 0:1],
                                                  rs[:, bass.ds(b * N + n, 1)], ALU.subtract, ALU.mult)
                ins.then_inc(h_ready, 1)

            def norm_columns(bank, count):
                dve.wait_ge(misc_full, count)
                nc.vector.tensor_scalar(hT[:, :], misc[bank][:, :], cols[:, 6:7], cols[:, 7:8], ALU.mult, ALU.add)\
                    .then_inc(misc_drained[bank], 1)

            def sums(b, bank, full, drained):
                dve.wait_ge(sc_drained[0], SC_MLP + b)
                dve.wait_ge(misc_full, full)
                nc.vector.scalar_tensor_tensor(out=r1, in0=misc[bank][:, :], scalar=dequant[:, 0:1],
                                               in1=x1_all[:, b, :, :].rearrange("p n d -> p (n d)"),
                                               op0=ALU.mult, op1=ALU.add).then_inc(misc_drained[bank], 1)
                dve.wait_ge(misc_drained[bank], drained)
                dve.wait_ge(resid_ready, b + 1)
                dve.wait_ge(sc_full, NSC * B + b + 1)
                nc.vector.tensor_tensor(r2, sc[0][:, 0:512], r1, ALU.add).then_inc(sc_drained[0], 1)

            norm_tokens(0)
            norm_columns(0, M_ALL + 1)
            with dve.Fori(0, B - 1) as b:
                norm_tokens(b + 1)
                norm_columns(1, M_ALL + 6 * b + 6)
                sums(b, 0, M_ALL + 6 * b + 7, b * 3 + M_ALL // 2 + 4)
            sums(B - 1, 1, M_ALL + 6 * B, 3 * B + M_ALL // 2)

        @block.tensor
        def _(pe):
            def open_misc(it, name):
                use = Use(*it, name)
                if it[0] != "start" or use.count_open > 0:
                    pe.wait_ge(use.drained, use.count_open)
                return use.bank

            def open_sc(b, use):
                u = SC_SLOT[use]
                pe.wait_ge(sc_drained[u % 2], b * (NSC // 2) + u // 2 + 1)
                return sc[u % 2]

            def open_acc(b, u):
                pe.wait_ge(acc_drained[u % 2], b * (N_ACC // 2) + u // 2 + 1)
                return acc[u % 2]

            def prepare(it, b):
                pe.wait_ge(xh_loaded, 16 * (b + 1))
                for k, name in enumerate(("xTa", "xTb")):
                    m = open_misc(it, name)
                    for n in range(N // 2):
                        ins = nc.tensor.transpose(m[:, n * C:(n + 1) * C], xh[:, k * N // 2 + n, :], ident[:, :])
                    ins.then_inc(misc_full, 1)
                for name in ("xTa", "xTb"):
                    wait_misc_drained(pe, it, name)

                def project(i):
                    m = open_misc(it, f"p{i}")
                    return nc.tensor.matmul(m[:, :], w_cols[:, i, :], xT[:, :], start=True, stop=True)\
                        .then_inc(misc_full, 1)

                project(KS)
                project(QS)
                natural(it, "vs", P)
                natural(it, "kn", 2 * P)
                project(QA)
                project(KA)

            def natural(it, name, o):
                m = open_misc(it, name)
                for n in range(N):
                    ins = nc.tensor.matmul(m[:, n * C:(n + 1) * C], xT[:, n * C:(n + 1) * C], w_nat[:, o:o + P],
                                           start=True, stop=True)
                ins.then_inc(misc_full, 1)

            def key_values(it, b, n):
                if n == 0:
                    pe.wait_ge(phi_ready, 3 * (b + 1))
                m = open_misc(it, f"kv{n}")
                nc.tensor.matmul(m[:, 0:H * (E + 1)], phi[:, 2, n * C:(n + 1) * C], v_s[:, n, :, 0:E + 1],
                                 start=True, stop=True).then_inc(misc_full, 1)

            def lin_scores(b, t):
                dst = open_sc(b, ("lin", t))
                n, h0 = t // 2, 8 * (t % 2)
                for hh in range(8):
                    ins = nc.tensor.matmul(dst[:, hh * C:(hh + 1) * C],
                                           stack[KS][0:KPAD, h0 + hh, n * C:(n + 1) * C],
                                           stack[QS][0:KPAD, h0 + hh, n * C:(n + 1) * C], start=True, stop=True)
                ins.then_inc(sc_full, 1)

            def max_scores(b, i):
                mc, h0, nh = SOFT[i]
                t = open_sc(b, ("max", i))
                w = 1024 // nh
                mask = mask_first[:, :, :] if mc == 0 else mask_win[:, :, :, :]
                for bank in range(2):
                    nc.tensor.matmul(t[:, bank * 512:(bank + 1) * 512], ident16[:, :], mask,
                                     start=True, stop=False, skip_group_check=True)
                    for hh in range(nh // 2):
                        hl = bank * nh // 2 + hh
                        ins = nc.tensor.matmul(t[:, hl * w:(hl + 1) * w],
                                               stack[QA][0:KPAD, h0 + hl, mc * C:(mc + 1) * C],
                                               stack[KA][0:KPAD, h0 + hl, (mc + 1) * C - w:(mc + 1) * C],
                                               start=False, stop=True, skip_group_check=True)
                ins.then_inc(sc_full, 1)

            def exp_scores(b, i):
                mc, h0, nh = SOFT[i]
                t = open_sc(b, ("exp", i))
                half = 8 // nh
                for hh in range(nh):
                    for w in range(half):
                        key = (mc - half + 1 + w) * C
                        o = (hh * half + w) * C
                        ins = nc.tensor.matmul(t[:, o:o + C], stack[KA][0:KPAD + CROWS, h0 + hh, key:key + C],
                                               stack[QA][0:KPAD + CROWS, h0 + hh, mc * C:(mc + 1) * C],
                                               start=True, stop=True)
                ins.then_inc(sc_full, 1)

            def lin_out(b, n):
                a = open_acc(b, n)
                for g in range(4):
                    cols_g = slice(g * C, (g + 1) * C)
                    if n:
                        pe.wait_ge(state_ready, 2 * b + max(n - 1, 1))
                        nc.tensor.matmul(a[:, cols_g], state[n - 1][:, 4 * g:4 * g + 4, :],
                                         phi[:, 0, n * C:(n + 1) * C], start=(g == 0), stop=False,
                                         skip_group_check=True)
                    t = 2 * n + g // 2
                    if g % 2 == 0:
                        pe.wait_ge(lin_masked, b * N_LIN + t + 1)
                    for j in range(4):
                        ins = nc.tensor.matmul(a[32 * j:32 * j + VW, cols_g], v_s[:, n, 4 * g + j, :],
                                               pa[t % PA][:, (4 * (g % 2) + j) * C:(4 * (g % 2) + j + 1) * C],
                                               start=(n == 0 and g == 0), stop=True, skip_group_check=True)
                ins.then_inc(acc_full, 1)

            def window_out(b, i):
                mc, h0, nh = SOFT[i]
                a = open_acc(b, N + mc) if h0 == 0 else acc[(N + mc) % 2]
                pe.wait_ge(masked, b * NT + i + 1)
                half = 8 // nh
                p = pa[(N_LIN + i) % PA]
                for g in range(nh // 4):
                    for w in range(half):
                        for j in range(4):
                            hh = 4 * g + j
                            o = (hh * half + w) * C
                            gg = (h0 + hh) // 4
                            ins = nc.tensor.matmul(
                                a[32 * j:32 * j + VW, gg * C:(gg + 1) * C],
                                v_a[:, mc - half + 1 + w, h0 + hh, :], p[:, o:o + C],
                                start=(gg == 0 and w == 0), stop=(w == half - 1), skip_group_check=True)
                ins.then_inc(pa_used, 1)

            def to_tokens(it, b, u):
                m = open_misc(it, unit(u) + "nat")
                pe.wait_ge(acc_drained[u % 2], b * (N_ACC // 2) + u // 2 + 2)
                for g in range(4):
                    ins = nc.tensor.transpose(m[:, g * C:(g + 1) * C], acc_s[u % 2][:, g * C:(g + 1) * C],
                                              ident[:, :])
                ins.then_inc(misc_full, 1)

            def to_columns(it, u):
                m = open_misc(it, unit(u) + "T")
                wait_misc_drained(pe, it, unit(u) + "nat")
                nc.tensor.transpose(m[:, 0:C], nat[u % 2][:, :], ident[:, :]).then_inc(misc_full, 1)

            def attend(it, b):
                more = it[0] == "loop"
                for i in (KS, QS):
                    pe.wait_ge(stacked[i], 16 * NPROD * (b + 1))
                for t in range(PA):
                    lin_scores(b, t)
                lin_out(b, 0)
                for i in (QA, KA):
                    pe.wait_ge(stacked[i], 16 * NPROD * (b + 1))
                for i in range(NT):
                    max_scores(b, i)
                    if PA + i < N_LIN:
                        lin_scores(b, PA + i)
                    if i == 1:
                        lin_out(b, 1)
                    if i == 3:
                        lin_out(b, 2)
                        to_tokens(it, b, 0)
                    if i == 5:
                        lin_out(b, 3)
                        to_tokens(it, b, 1)
                    if i in (7, 9):
                        to_tokens(it, b, (i - 3) // 2)
                    if i in (6, 8, 10, 11):
                        to_columns(it, {6: 0, 8: 1, 10: 2, 11: 3}[i])
                wait_sc_drained(pe, b, ("max", NT - 2))
                wait_sc_drained(pe, b, ("max", NT - 1))
                m = open_misc(it, "cT")
                for n in range(N):
                    ins = nc.tensor.transpose(m[0:H, n * C:(n + 1) * C], negc[:, n, :], ident[:, :])
                ins.then_inc(misc_full, 1)
                if more:
                    prepare(it, b + 1)
                pe.wait_ge(c_stacked, 16 * CROWS * (b + 1))
                for i in range(NT + LAG + 6):
                    if i < NT:
                        exp_scores(b, i)
                    if not more and i == 3:
                        pe.wait_ge(amax_ready, 1)
                        m = open_misc(it, "am")
                        for k in range(2):
                            ins = nc.tensor.transpose(m[0:1, k * P:(k + 1) * P], am[:, k:k + 1], ident[:, :])
                        ins.then_inc(misc_full, 1)
                    if LAG <= i < NT + LAG:
                        window_out(b, i - LAG)
                    if more and i == NT + LAG:
                        natural(it, "va", 0)
                    for mc in range(N):
                        if i == LAST_TILE[mc] + LAG + 2:
                            to_tokens(it, b, N + mc)
                        if i == LAST_TILE[mc] + LAG + 4:
                            to_columns(it, N + mc)
                    if not more and i == LAST_TILE[0] + LAG + 5:
                        pe.wait_ge(amax_ready, 2)
                        m = open_misc(it, "amb")
                        nc.tensor.matmul(m[:, 0:2], ones[0:1, :], am1[:, :], start=True, stop=True)\
                            .then_inc(misc_full, 1)
                    if more and i == NT + LAG + 2:
                        key_values(it, b + 1, 0)
                        key_values(it, b + 1, 1)
                if more:
                    key_values(it, b + 1, 2)
                m = open_misc(it, "mix")
                wait_misc_drained(pe, it, f"s{N - 1}T")
                for n in range(N):
                    pe_cols = slice(n * C, (n + 1) * C)
                    nc.tensor.matmul(m[:, pe_cols], oT[:, 0, pe_cols], w_mix[:, 1, :], start=True, stop=False)
                    ins = nc.tensor.matmul(m[:, pe_cols], oT[:, 1, pe_cols], w_mix[:, 0, :], start=False, stop=True)
                ins.then_inc(misc_full, 1)

            pe.wait_ge(ident_ready, 1)
            pe.wait_ge(early_loaded, EARLY_ALL)
            start = ("start", 0)
            prepare(start, 0)
            pe.wait_ge(late_loaded, LATE_ALL)
            for k in range(2):
                nc.tensor.transpose(sc[k][:, 0:P], wp[:, k, :], ident[:, :]).then_inc(pre_full, 1)
            for k in range(2):
                pe.wait_ge(sc_drained[k], 1)
                ins = nc.tensor.matmul(acc[0][:, k * P:(k + 1) * P], wpT[:, k, :], wo[:, :], start=True, stop=True)
            ins.then_inc(pre_full, 1)
            pe.wait_ge(pre_ready, 1)
            nc.tensor.matmul(acc[1][:, 0:P], pre, wo[:, :], start=True, stop=True).then_inc(pre_full, 1)
            pe.wait_ge(const_ready, CONST_ALL)
            natural(start, "va", 0)
            for n in range(N - 1):
                key_values(start, 0, n)

            with pe.Fori(0, B - 1) as b:
                attend(("loop", b), b)
            attend(("end", B - 1), B - 1)

            for t in range(B + 1):
                pe.wait_ge(quantised, t + 1)
                pe.wait_ge(sc_drained[t % 2], 1 + B * (NSC // 2) + t // 2)
                turned = sc[t % 2][:, 0:256].bitcast(BF16)
                if t < B:
                    for n in range(N):
                        ins = nc.tensor.transpose(turned[:, n * C:(n + 1) * C], xq[:, t, n * C:(n + 1) * C],
                                                  ident16[:, :])
                else:
                    ins = nc.tensor.transpose(turned[:, 0:P], wq[:, :], ident16[:, :])
                ins.then_inc(pre_full, 1)

            def turn_tokens(b, bank, opened):
                pe.wait_ge(h_ready, b + 1)
                pe.wait_ge(misc_drained[bank], opened)
                for n in range(N):
                    ins = nc.tensor.transpose(misc[bank][:, n * C:(n + 1) * C], hn[:, n, :], ident[:, :])
                ins.then_inc(misc_full, 1)

            def mlp(b, more):
                half = b * 3 + M_ALL // 2
                for k in range(FC):
                    bank = (k + 1) % 2
                    pe.wait_ge(misc_drained[bank], half + (k + 1) // 2)
                    nc.tensor.matmul(misc[bank][:, :], w1[:, k * P:(k + 1) * P], hT[:, :], start=True, stop=True)\
                        .then_inc(misc_full, 1)
                if more:
                    turn_tokens(b + 1, 1, half + 2)
                bank, opened = (0, half + 3) if more else (1, half + 2)
                pe.wait_ge(misc_drained[bank], opened)
                for n in range(N):
                    ins = nc.tensor.matmul(misc[bank][:, n * C:(n + 1) * C], xqT_all[:, bass.ds(b * L + n * C, C)],
                                           wqT[:, :], start=True, stop=True)
                ins.then_inc(misc_full, 1)
                pe.wait_ge(misc_drained[0], half + 3)
                pe.wait_ge(sc_drained[0], SC_MLP + b)
                for n in range(N):
                    for k in range(FC):
                        ins = nc.tensor.matmul(sc[0][:, n * C:(n + 1) * C], hid[:, k, n * C:(n + 1) * C],
                                               w2[:, k, :], start=(k == 0), stop=(k == FC - 1))
                ins.then_inc(sc_full, 1)

            turn_tokens(0, 0, M_ALL // 2)
            pe.wait_ge(sc_drained[0], SC_MLP)
            pe.wait_ge(sc_drained[1], SC_MLP - 1)
            pe.wait_ge(misc_drained[0], M_ALL // 2 + 1)
            with pe.Fori(0, B - 1) as b:
                mlp(b, True)
            mlp(B - 1, False)


_INS = ["x", "g1", "b1", "Wqkv_a", "bqkv_a", "Wp_a", "bp_a", "Wqkv_s", "bqkv_s", "Wo_s", "bo_s", "Wo", "bo",
        "gm", "bm", "W1", "b1m", "W2", "b2m"]
_INS = ["L0_attn_" + n for n in _INS] + ["L0_ffn_weight", "L0_ffn_bias"]


def kernel(**inputs):
    import numpy as _np
    import concourse.bacc as _bacc
    from concourse.bass_utils import run_bass_kernel_spmd as _run

    nc = _bacc.Bacc("TRN2", target_bir_lowering=False, num_devices=1)
    arrays, args = {}, []
    for name in _INS:
        a = _np.ascontiguousarray(inputs[name])
        arrays[name] = a
        args.append(nc.dram_tensor(name, a.shape, F32, kind="ExternalInput").ap())
    shape = arrays["L0_attn_x"].shape
    args.append(nc.dram_tensor("out", shape, F32, kind="ExternalOutput").ap())
    attention_block_kernel(nc, *args)
    r = _run(nc, [arrays], core_ids=[0])
    return r.results[0]["out"]
```

```python
from contextlib import ExitStack

import concourse.bass as bass
from concourse import mybir

P = 128
H = 16
E = 8
C = 128
VW = 32
NPROD = 6
KROWS = NPROD * E
CROWS = 3
KPAD = 96
NEG = -1e30
LN_EPS = 1e-5
DEN_EPS = 1e-6
ELU_SHIFT = 1e-4
FP8_MAX = 448.0
AMAX_MIN = 1e-12
FP8_MIN_NORMAL = 2.0 ** -6
FP8_ROUND = 1.5 * 2.0 ** 20
EXPONENT_BITS = 0x7F800000

ALU = mybir.AluOpType
ACT = mybir.ActivationFunctionType
BF16 = mybir.dt.bfloat16
F32 = mybir.dt.float32
I32 = mybir.dt.int32
U32 = mybir.dt.uint32
AX_X = mybir.AxisListType.X

QA, KA, QS, KS = range(4)


def attention_block_kernel(nc, x, g1, b1, Wqkv_a, bqkv_a, Wp_a, bp_a, Wqkv_s, bqkv_s, Wo_s, bo_s,
                           Wo, bo, gm, bm, W1, b1m, W2, b2m, ffn_w, ffn_b, out):
    B, L, D = x.shape
    N = L // C
    F = W1.shape[1]
    FC = F // P
    SCALE = float(E) ** -0.5
    assert D == P and H * E == D and B % 2 == 0

    RUNS = [(0, 3), (3, 2), (5, 1)]
    QUERIES = (QA, QS)

    SOFT = [(0, 0, 8), (0, 8, 8)] + [(m, 4 * g, 4) for m in range(1, N) for g in range(4)]
    NT = len(SOFT)
    LAST_TILE = {m: max(i for i, t in enumerate(SOFT) if t[0] == m) for m in range(N)}

    PREP_LINEAR = ["xTa", "xTb", f"p{KS}", f"p{QS}"]
    PREP_REST = [f"p{QA}", f"p{KA}", "vs", "kn"]
    LINEAR = ["l1nat", "l0T", "cTa", "l2nat", "l1T", "l3nat", "l2T", "l3T", "cTb"]
    MISC = {
        "start": PREP_LINEAR + PREP_REST + ["va", "kv0", "kv12", "pre"],
        "loop": PREP_LINEAR[:3] + ["l0nat"] + PREP_LINEAR[3:] +
                ["l1nat", "l0T", "cTa", f"p{QA}", "l2nat", "l1T", f"p{KA}", "l3nat", "l2T", "l3T", "cTb",
                 "vs", "kn", "s0nat", "s0T", "s1nat", "s1T", "s2nat", "s2T", "va", "s3nat", "kv0", "s3T", "kv12", "mix"],
        "end": ["l0nat"] + LINEAR + ["amb", "s0nat", "s0T", "s1nat", "s1T", "s2nat", "s2T", "s3nat", "s3T", "mix"],
    }
    SLOT = {stage: {name: i for i, name in enumerate(names)} for stage, names in MISC.items()}
    M_START, M_LOOP, M_END = len(MISC["start"]), len(MISC["loop"]), len(MISC["end"])
    M_ALL = M_START + (B - 1) * M_LOOP + M_END
    assert M_START % 2 == M_LOOP % 2 == M_END % 2 == 0
    PA = 4
    N_LIN = 2 * N
    SC_ORDER = [("lin", i) for i in range(PA)]
    for i in range(NT):
        SC_ORDER += [("max", i)] + ([("lin", PA + i)] if PA + i < N_LIN else [])
    SC_ORDER += [("exp", i) for i in range(NT)]
    SC_SLOT = {use: i for i, use in enumerate(SC_ORDER)}
    NSC = len(SC_ORDER)
    assert NSC % 2 == 0
    N_ACC = 2 * N
    LAG = 3
    DVE_MASKS = (5, 8, 11)
    KEEP = 3e38

    with ExitStack() as ctx:
        def sb(name, shape, dt=F32):
            return ctx.enter_context(nc.sbuf_tensor(name, shape, dt))

        def sem(name):
            return ctx.enter_context(nc.semaphore(name))

        ident = sb("ident", [P, P])
        ident16 = sb("ident16", [P, P], BF16)
        mask_win = sb("mask_win", [P, 2, 2, C], BF16)
        mask_first = sb("mask_first", [P, 4, C], BF16)
        window = sb("window", [P, 2, C])
        own_head = sb("own_head", [P, H, E + 1])
        ones = sb("ones", [P, P])
        w_cols = sb("w_cols", [P, 4, P])
        w_nat = sb("w_nat", [P, 3 * P])
        wo = sb("wo", [P, P])
        w_mix = sb("w_mix", [P, 2, P])
        w1 = sb("w1", [P, F])
        w2 = sb("w2", [P, FC, P])
        wf = sb("wf", [P, P])
        wqT = sb("wqT", [P, P], BF16)
        cols = sb("cols", [P, 10])
        gb = sb("gb", [P, 4])
        b1c = sb("b1c", [P, FC])
        b_nat = sb("b_nat", [P, 3 * P])
        b_out = sb("b_out", [P, P])
        b_mix = sb("b_mix", [P, P])
        xn_all = sb("xn_all", [P, B, N, P])
        xh_all = sb("xh_all", [P, B, N, P])
        xq = sb("xq", [P, B, L], BF16)
        wq = sb("wq", [P, P], BF16)
        st_all = sb("st_all", [P, B, N, 6])
        xqT_all = sb("xqT_all", [P, B * N * P], BF16)
        mv = sb("mv", [P, B * N, 2])
        var = sb("var", [P, B * N])
        sd = sb("sd", [P, B * N])
        rs = sb("rs", [P, B * N])
        rt = sb("rt", [P, B * N])
        shift = sb("shift", [P, B * N])
        warm = sb("warm", [P, 1])
        pre_col = sb("pre_col", [P, 1])
        am = sb("am", [P, 2])
        am1 = sb("am1", [1, 2])
        amb = sb("amb", [P, 2])
        fscale = sb("fscale", [P, 2])
        finv = sb("finv", [P, 2])
        dequant = sb("dequant", [P, 1])
        xh = sb("xh", [P, N, P])
        xT = sb("xT", [P, L])
        f = sb("f", [P, 4, L])
        parts = [sb(f"parts{i}", [P, 3, L], BF16) for i in range(4)]
        rest = sb("rest", [P, 4, L])
        stack = [sb(f"stack{i}", [P, H, L], BF16) for i in range(4)]
        v_a = sb("v_a", [P, N, H, VW])
        v_s = sb("v_s", [P, N, H, VW])
        k_lin = sb("k_lin", [P, L])
        phi = sb("phi", [P, 3, L])
        negc = sb("negc", [P, N, H])
        c_f = sb("c_f", [H, L])
        c_parts = sb("c_parts", [H, 3, L], BF16)
        kv_new = sb("kv_new", [P, H, E + 1])
        state = [sb(f"state{n}", [P, H, VW]) for n in range(1, N)]
        pa_all = sb("pa_all", [P, PA, 2 * 512])
        pa = [pa_all[:, i, :] for i in range(PA)]
        acc_s = [sb(f"acc_s{i}", [P, 512]) for i in range(2)]
        den = sb("den", [P, H])
        rden = sb("rden", [P, H])
        nat = [sb(f"nat{i}", [P, P]) for i in range(2)]
        oT = sb("oT", [P, 2, L])
        x1_all = xh_all
        c_rest = rest[0:H, 0, :]
        wp = pa_all[:, 2, 0:2 * P].rearrange("p (a d) -> p a d", a=2)
        wpT = pa_all[:, 2, 2 * P:4 * P].rearrange("p (a d) -> p a d", a=2)
        b_out2 = acc_s[0][:, 0:2 * P].rearrange("p (a d) -> p a d", a=2)
        bo_rows = acc_s[0][:, 2 * P:3 * P]
        pre = acc_s[1][:, 0:P]
        hn = xh
        hT = xT
        hid = f
        r1 = phi[:, 0, :]
        r2 = phi[:, 1, :]
        r3 = phi[:, 2, :]
        o_sb = k_lin
        q_e = rest

        sc = [ctx.enter_context(nc.psum_tensor(f"sc{i}", [P, 1024], F32)) for i in range(2)]
        acc = [ctx.enter_context(nc.psum_tensor(f"acc{i}", [P, 512], F32)) for i in range(2)]
        misc = [ctx.enter_context(nc.psum_tensor(f"misc{i}", [P, 512], F32)) for i in range(2)]

        x_loaded = [sem(f"x_loaded{b}") for b in range(B)]
        early_loaded = sem("early_loaded")
        late_loaded = sem("late_loaded")
        const_set = sem("const_set")
        ident_ready = sem("ident_ready")
        const_ready = sem("const_ready")
        out_bias_ready = sem("out_bias_ready")
        stacks_cleared = sem("stacks_cleared")
        dve_step = sem("dve_step")
        var_ready = sem("var_ready")
        sd_ready = sem("sd_ready")
        shift_ready = sem("shift_ready")
        xh_ready = sem("xh_ready")
        bias_ready = sem("bias_ready")
        pre_ready = sem("pre_ready")
        pre_full = sem("pre_full")
        amax_ready = sem("amax_ready")
        quantised = sem("quantised")
        xh_loaded = sem("xh_loaded")
        misc_full = sem("misc_full")
        sc_full = sem("sc_full")
        acc_full = sem("acc_full")
        pool_step = sem("pool_step")
        c_copied = sem("c_copied")
        part_copied = sem("part_copied")
        rest_ready = sem("rest_ready")
        min_ready = sem("min_ready")
        exp_ready = sem("exp_ready")
        phi_ready = sem("phi_ready")
        state_ready = sem("state_ready")
        pa_used = sem("pa_used")
        tiles_taken = sem("tiles_taken")
        loads_begun = sem("loads_begun")
        lin_masked = sem("lin_masked")
        masked = sem("masked")
        dve_masked = sem("dve_masked")
        h_ready = sem("h_ready")
        resid_ready = sem("resid_ready")
        resid_begun = sem("resid_begun")
        warm_ready = sem("warm_ready")
        x_again = sem("x_again")
        stored = sem("stored")
        c_ready = [sem(f"c_ready{i}") for i in range(2)]
        c_stacked = [sem(f"c_stacked{i}") for i in range(2)]
        misc_drained = [sem("misc_drained0"), sem("misc_drained1")]
        sc_drained = [sem("sc_drained0"), sem("sc_drained1")]
        acc_drained = [sem("acc_drained0"), sem("acc_drained1")]
        parts_ready = [sem(f"parts_ready{i}") for i in range(4)]
        scratch_written = [sem(f"scratch_written{i}") for i in range(4)]
        stacked = [sem(f"stacked{i}") for i in range(4)]
        scratch = [nc.dram_tensor(f"scratch{i}", (3, E, H, L), BF16, kind="Internal").ap() for i in range(4)]
        x_dram = x.rearrange("b (n p) d -> b p n d", p=P)
        out_dram = out.rearrange("b (n p) d -> b p n d", p=P)

        early_cols = [
            (cols[:, 4:5], g1), (cols[:, 5:6], b1), (cols[:, 0:2], bqkv_a[0:2 * P]), (cols[:, 2:4], bqkv_s[0:2 * P]),
        ]
        early = [
            (w_cols[:, KS, :], Wqkv_s[:, P:2 * P]), (w_cols[:, QS, :], Wqkv_s[:, 0:P]),
            (w_nat[:, P:2 * P], Wqkv_s[:, 2 * P:3 * P]), (w_nat[:, 2 * P:3 * P], Wqkv_s[:, P:2 * P]),
            (w_cols[:, QA, :], Wqkv_a[:, 0:P]), (w_cols[:, KA, :], Wqkv_a[:, P:2 * P]),
            (w_nat[:, 0:P], Wqkv_a[:, 2 * P:3 * P]),
            (b_nat[:, P:2 * P], bqkv_s[2 * P:3 * P].partition_broadcast(P)),
            (b_nat[:, 2 * P:3 * P], bqkv_s[P:2 * P].partition_broadcast(P)),
            (b_nat[:, 0:P], bqkv_a[2 * P:3 * P].partition_broadcast(P)),
        ]
        late = [
            (wp[:, 0, :], Wp_a), (wp[:, 1, :], Wo_s), (wo[:, :], Wo),
            (bo_rows, bo.partition_broadcast(P)),
            (b_out2[:, 0, :], b2m.partition_broadcast(P)), (b_out2[:, 1, :], ffn_b.partition_broadcast(P)),
            (w1[:, :], W1), (w2[:, :, :], W2.rearrange("(k p) d -> p k d", p=P)), (wf[:, :], ffn_w),
        ]
        late_cols = [(cols[:, 6:7], gm), (cols[:, 7:8], bm), (cols[:, 8:9], bp_a), (cols[:, 9:10], bo_s),
                  (b1c[:, :], b1m)]
        EARLY_ALL = 16 * (len(early) + len(early_cols))
        LATE_ALL = 16 * (len(late) + len(late_cols))
        PRE_FULL = 4
        SC_MLP = 1 + B * (NSC // 2) + 2
        CONST_EARLY = 5
        CONST_ALL = 10

        class Use:

            def __init__(self, stage, b, name):
                slot = SLOT[stage][name]
                before = {"start": 0, "loop": M_START, "end": M_START + (B - 1) * M_LOOP}[stage]
                self.parity = slot % 2
                self.bank = misc[slot % 2]
                self.drained = misc_drained[slot % 2]
                if stage == "loop":
                    self.count_full = b * M_LOOP + (before + slot + 1)
                    self.count_open = b * (M_LOOP // 2) + (before // 2 + slot // 2)
                else:
                    self.count_full = before + slot + 1
                    self.count_open = before // 2 + slot // 2
                self.count_drained = self.count_open + 1

        def wait_misc_full(eng, it, name):
            eng.wait_ge(misc_full, Use(*it, name).count_full)

        def wait_misc_drained(eng, it, name):
            use = Use(*it, name)
            eng.wait_ge(use.drained, use.count_drained)

        def sc_of(use):
            return sc[SC_SLOT[use] % 2]

        def wait_sc_full(eng, b, use):
            eng.wait_ge(sc_full, b * NSC + SC_SLOT[use] + 1)

        def wait_sc_drained(eng, b, use):
            u = SC_SLOT[use]
            eng.wait_ge(sc_drained[u % 2], b * (NSC // 2) + u // 2 + 2)

        def unit(u):
            return f"{'ls'[u // N]}{u % N}"

        def apart(eng):
            eng.wait_ge(const_ready, 1)

        block = ctx.enter_context(nc.Block())

        @block.sync
        def _(sp):
            sp.dma_start(xn_all[:, 0, :, :], x_dram[0]).then_inc(x_loaded[0], 16)
            for dst, src in early:
                sp.dma_start(dst, src).then_inc(early_loaded, 16)
            for b in range(1, B):
                sp.dma_start(xn_all[:, b, :, :], x_dram[b]).then_inc(x_loaded[b], 16)
            for dst, src in late:
                sp.dma_start(dst, src).then_inc(late_loaded, 16)
            for dst, src in late_cols:
                sp.dma_start(dst, src.rearrange("(k p) -> p k", p=P), allow_slow_non_contiguous=True)\
                  .then_inc(late_loaded, 16)

            def load_tokens(b):
                apart(sp)
                sp.wait_ge(xh_ready, b + 1)
                sp.dma_start(xh[:, :, :], xh_all[:, b, :, :]).then_inc(xh_loaded, 16)

            def write_parts(i, b, first=False):
                apart(sp)
                sp.wait_ge(parts_ready[i], b + 1)
                if b is not 0:
                    sp.sem_inc(loads_begun, 1)
                    sp.wait_ge(stacked[i], 16 * len(RUNS) * b)
                for part in range(3):
                    sp.dma_start(scratch[i][part].rearrange("e h t -> h e t"), parts[i][:, part, :])\
                      .then_inc(scratch_written[i], 16)

            def load_stack(i, b):
                apart(sp)
                sp.wait_ge(scratch_written[i], 16 * 3 * (b + 1))
                for run, (g, n) in enumerate(RUNS):
                    if i in QUERIES:
                        src = scratch[i][run:run + 1].rearrange("a e h t -> a e (h t)").to_broadcast([n, E, H * L])
                    else:
                        src = scratch[i][0:n].rearrange("a e h t -> (a e) (h t)")
                    sp.dma_start(stack[i][g * E:(g + n) * E, :, :].rearrange("r h t -> r (h t)"), src)\
                      .then_inc(stacked[i], 16)

            def load_maxima(b, half):
                apart(sp)
                sp.wait_ge(c_ready[half], b + 1)
                tokens = slice(half * L // 2, (half + 1) * L // 2)
                for r in range(CROWS):
                    sp.dma_start(stack[QA][KPAD + r:KPAD + r + 1, :, tokens], c_parts[:, r, tokens])\
                      .then_inc(c_stacked[half], 16)

            sp.wait_ge(stacks_cleared, 4)
            for pair in ((KS, QS), (QA, KA)):
                for i in pair:
                    write_parts(i, 0, first=True)
                for i in pair:
                    if i in (KS, QS):
                        load_stack(i, 0)
            with sp.Fori(0, B - 1) as b:
                load_tokens(b + 1)
                for i in (QA, KA):
                    load_stack(i, b)
                load_maxima(b, 0)
                write_parts(KS, b + 1)
                load_maxima(b, 1)
                write_parts(QS, b + 1)
                apart(sp)
                wait_sc_full(sp, b, ("lin", N_LIN - 1))
                sp.sem_inc(loads_begun, 1)
                for i in (KS, QS):
                    load_stack(i, b + 1)
                for i in (QA, KA):
                    write_parts(i, b + 1)
                apart(sp)
                wait_sc_full(sp, b, ("exp", NT - 1))
                sp.sem_inc(loads_begun, 1)
            for i in (QA, KA):
                load_stack(i, B - 1)
            for half in range(2):
                load_maxima(B - 1, half)
            sp.wait_ge(misc_full, M_ALL)
            r3_rows = r3.rearrange("p (n d) -> p n d", d=P)
            sp.dma_start(r3_rows, x_dram[0]).then_inc(x_again, 16)
            with sp.Fori(0, B - 1) as b:
                apart(sp)
                sp.wait_ge(sc_drained[1], SC_MLP + b + 1)
                sp.dma_start(out_dram[b], o_sb[:, :].rearrange("p (n d) -> p n d", d=P)).then_inc(stored, 16)
                apart(sp)
                sp.wait_ge(stored, 16 * b + 16)
                sp.dma_start(r3_rows, x_dram[b + 1]).then_inc(x_again, 16)
            sp.wait_ge(sc_drained[1], SC_MLP + B)
            sp.dma_start(out_dram[B - 1], o_sb[:, :].rearrange("p (n d) -> p n d", d=P)).then_inc(stored, 16)
            sp.wait_ge(stored, 16 * B)

        @block.gpsimd
        def _(pool):
            pool.memset(warm[:, :], 1.0).then_inc(warm_ready, 1)
            pool.memset(ident[:, :], 0.0).then_inc(const_set, 1)
            pool.wait_ge(const_set, 1)
            pool.affine_select(out=ident[:, :], in_=ident[:, :], pattern=[[-1, P]], compare_op=ALU.not_equal,
                               fill=1.0, base=0, channel_multiplier=1).then_inc(ident_ready, 1)
            small = ((v_s, 0.0), (v_a, 0.0), (own_head, 1.0), (ones, 1.0), (ident16, 0.0), (mask_win, 0.0),
                     (mask_first, 0.0), (window, KEEP)) + tuple((s, 0.0) for s in state)
            for tile, value in small:
                pool.memset(tile[tuple(slice(None) for _ in tile.shape)], value).then_inc(const_set, 1)
            for i, word in ((KS, 0), (QS, 0), (QA, 0), (KA, 0x3F803F80)):
                pool.memset(stack[i][:, :, :].rearrange("p h t -> p (h t)").bitcast(U32), word)\
                    .then_inc(stacks_cleared, 1)
            pool.wait_ge(const_set, 1 + len(small))
            for v in (v_s, v_a):
                pool.memset(v[:, :, :, E:E + 1], 1.0).then_inc(const_ready, 1)
            pool.affine_select(out=ident16[:, :], in_=ident16[:, :], pattern=[[-1, P]], compare_op=ALU.not_equal,
                               fill=1.0, base=0, channel_multiplier=1).then_inc(const_ready, 1)
            pool.affine_select(out=own_head[:, :, :], in_=own_head[:, :, :], pattern=[[-E, H], [0, E + 1]],
                               compare_op=ALU.is_ge, fill=0.0, base=0, channel_multiplier=1)\
                .then_inc(const_ready, 1)
            pool.wait_ge(const_ready, 4)
            pool.affine_select(out=own_head[:, :, :], in_=own_head[:, :, :], pattern=[[E, H], [0, E + 1]],
                               compare_op=ALU.is_ge, fill=0.0, base=E - 1, channel_multiplier=-1)\
                .then_inc(const_ready, 1)
            pool.affine_select(out=mask_win[:, :, 0, :], in_=mask_win[:, :, 0, :], pattern=[[0, 2], [1, C]],
                               compare_op=ALU.is_gt, fill=NEG, base=0, channel_multiplier=-1)\
                .then_inc(const_ready, 1)
            pool.affine_select(out=mask_win[:, :, 1, :], in_=mask_win[:, :, 1, :], pattern=[[0, 2], [-1, C]],
                               compare_op=ALU.is_ge, fill=NEG, base=0, channel_multiplier=1)\
                .then_inc(const_ready, 1)
            pool.affine_select(out=mask_first[:, :, :], in_=mask_first[:, :, :], pattern=[[0, 4], [-1, C]],
                               compare_op=ALU.is_ge, fill=NEG, base=0, channel_multiplier=1)\
                .then_inc(const_ready, 1)
            pool.affine_select(out=window[:, 0, :], in_=window[:, 0, :], pattern=[[-1, C]],
                               compare_op=ALU.is_gt, fill=0.0, base=0, channel_multiplier=1).then_inc(const_ready, 1)
            pool.affine_select(out=window[:, 1, :], in_=window[:, 1, :], pattern=[[1, C]],
                               compare_op=ALU.is_ge, fill=0.0, base=0, channel_multiplier=-1)\
                .then_inc(const_ready, 1)
            for k, i in enumerate((QA, KA)):
                pool.wait_ge(part_copied, k + 1)
                pool.tensor_tensor(rest[:, i, :], f[:, i, :], parts[i][:, 0, :], ALU.subtract).then_inc(rest_ready, 1)
            for k, i in enumerate((QA, KA)):
                pool.wait_ge(part_copied, k + 3)
                pool.tensor_tensor(parts[i][:, 2, :], rest[:, i, :], parts[i][:, 1, :], ALU.subtract)\
                    .then_inc(parts_ready[i], 1)
            pool.wait_ge(late_loaded, LATE_ALL)
            pool.tensor_tensor(b_out[:, :], b_out2[:, 0, :], b_out2[:, 1, :], ALU.add).then_inc(out_bias_ready, 1)

            def split_maxima(it, b):
                tokens = slice(0, L // 2)
                wait_misc_drained(pool, it, "cTa")
                pool.sem_inc(tiles_taken, 1)
                pool.tensor_copy(c_parts[:, 0, tokens], c_f[:, tokens]).then_inc(pool_step, 1)
                pool.wait_ge(pool_step, 3 * b + 1)
                pool.tensor_tensor(c_rest[:, tokens], c_f[:, tokens], c_parts[:, 0, tokens], ALU.subtract)\
                    .then_inc(pool_step, 1)
                pool.wait_ge(pool_step, 3 * b + 2)
                pool.sem_inc(tiles_taken, 1)
                pool.tensor_copy(c_parts[:, 1, tokens], c_rest[:, tokens]).then_inc(pool_step, 1)
                pool.wait_ge(pool_step, 3 * b + 3)
                pool.tensor_tensor(c_parts[:, 2, tokens], c_rest[:, tokens], c_parts[:, 1, tokens], ALU.subtract)\
                    .then_inc(c_ready[0], 1)

            def masks(it, b, by_dve):
                for t in range(N_LIN):
                    wait_sc_drained(pool, b, ("lin", t))
                    pool.sem_inc(tiles_taken, 1)
                    p = pa[t % PA].rearrange("p (h r) -> p h r", r=C)
                    pool.affine_select(out=p, in_=p, pattern=[[0, 8], [1, C]], compare_op=ALU.is_ge,
                                       fill=0.0, base=0, channel_multiplier=-1).then_inc(lin_masked, 1)
                split_maxima(it, b)
                for i, (m, h0, nh) in enumerate(SOFT):
                    if i in by_dve:
                        continue
                    wait_sc_drained(pool, b, ("exp", i))
                    pool.sem_inc(tiles_taken, 1)
                    k = (N_LIN + i) % PA
                    if m == 0:
                        p = pa[k].rearrange("p (h r) -> p h r", r=C)
                        pool.affine_select(out=p, in_=p, pattern=[[0, nh], [1, C]], compare_op=ALU.is_ge,
                                           fill=0.0, base=0, channel_multiplier=-1).then_inc(masked, 1)
                    else:
                        p = pa[k].rearrange("p (h w r) -> p h w r", w=2, r=C)
                        pool.affine_select(out=p[:, :, 0, :], in_=p[:, :, 0, :], pattern=[[0, nh], [-1, C]],
                                           compare_op=ALU.is_gt, fill=0.0, base=0, channel_multiplier=1)
                        pool.affine_select(out=p[:, :, 1, :], in_=p[:, :, 1, :], pattern=[[0, nh], [1, C]],
                                           compare_op=ALU.is_ge, fill=0.0, base=0, channel_multiplier=-1)\
                            .then_inc(masked, 1)

            with pool.Fori(0, B - 1) as b:
                masks(("loop", b), b, DVE_MASKS)
            masks(("end", B - 1), B - 1, ())

            pool.wait_ge(out_bias_ready, 1)
            def residual(b, bank, drained):
                pool.wait_ge(x_again, 16 * (b + 1))
                pool.tensor_tensor(r3.rearrange("p (n d) -> p n d", d=P), r3.rearrange("p (n d) -> p n d", d=P),
                                   b_out[:, :].rearrange("p (a d) -> p a d", a=1).to_broadcast([P, N, P]),
                                   ALU.add).then_inc(resid_begun, 1)
                pool.wait_ge(resid_begun, b + 1)
                pool.wait_ge(misc_drained[bank], drained)
                pool.tensor_tensor(r2, r1, r3, ALU.add).then_inc(resid_ready, 1)

            with pool.Fori(0, B - 1) as b:
                residual(b, 0, b * 3 + M_ALL // 2 + 4)
            residual(B - 1, 1, 3 * B + M_ALL // 2)

        @block.scalar
        def _(act):
            def root(j, first, last):
                tokens = slice(first * N, last * N)
                act.wait_ge(var_ready, j)
                nc.scalar.activation(sd[:, tokens], var[:, tokens], ACT.Sqrt).then_inc(sd_ready, 1)

            def second_norm(j, first, last):
                act.wait_ge(shift_ready, j)
                for b in range(first, last):
                    for n in range(N):
                        t = b * N + n
                        dst = xh_all[:, b, n, :] if b else xh[:, n, :]
                        ins = nc.scalar.activation(dst, xn_all[:, b, n, :], ACT.Identity,
                                                   scale=rs[:, t:t + 1], bias=shift[:, t:t + 1])
                    ins.then_inc(xh_ready, 1)

            def drain(it, name, dst, src, func=ACT.Copy, **kw):
                use = Use(*it, name)
                act.wait_ge(misc_full, use.count_full)
                nc.scalar.activation(dst, use.bank[src], func, **kw).then_inc(use.drained, 1)

            def turned(it, k):
                half = L // 2
                drain(it, ("xTa", "xTb")[k], xT[:, k * half:(k + 1) * half], (slice(None), slice(0, half)),
                      ACT.Identity, scale=cols[:, 4:5], bias=cols[:, 5:6])

            def project(it, b, i):
                if it[0] != "start":
                    act.wait_ge(parts_ready[i], b)
                drain(it, f"p{i}", f[:, i, :], (slice(None), slice(None)), ACT.Identity,
                      scale=SCALE if i in (QA, QS) else 1.0, bias=gb[:, i:i + 1])

            def exp_min(b, c):
                j = (1, 0, 2)[c]
                act.wait_ge(min_ready, 3 * b + c + 1)
                nc.scalar.activation(phi[:, j, :], phi[:, j, :], ACT.Exp).then_inc(exp_ready, 1)

            def copy_lin(b, t):
                wait_sc_full(act, b, ("lin", t))
                if t >= PA:
                    act.wait_ge(acc_full, b * N + (t - PA) // 2 + 1)
                nc.scalar.activation(pa[t % PA], sc_of(("lin", t))[:, :], ACT.Copy)\
                    .then_inc(sc_drained[SC_SLOT["lin", t] % 2], 1)

            def save_acc(it, b, u):
                if u < N:
                    act.wait_ge(acc_full, b * N + u + 1)
                else:
                    act.wait_ge(pa_used, b * NT + LAST_TILE[u - N] + 1)
                if u >= 2:
                    wait_misc_full(act, it, unit(u - 2) + "nat")
                nc.scalar.activation(acc_s[u % 2][:, :], acc[u % 2][:, :], ACT.Copy)\
                    .then_inc(acc_drained[u % 2], 1)

            def save_T(it, u):
                kind, n = u // N, u % N
                drain(it, unit(u) + "T", oT[:, kind, n * C:(n + 1) * C], (slice(None), slice(0, C)))

            def copy_maxima(it, half):
                use = Use(*it, ("cTa", "cTb")[half])
                act.wait_ge(misc_full, use.count_full)
                sem_done = c_copied if it[0] == "end" and half else use.drained
                nc.scalar.activation(c_f[:, half * L // 2:(half + 1) * L // 2], use.bank[0:H, 0:L // 2], ACT.Copy)\
                    .then_inc(sem_done, 1)

            def attend(it, b):
                more = it[0] == "loop"
                for t in range(PA):
                    copy_lin(b, t)
                    if more and t in (1, 3):
                        turned(it, t // 2)
                copy_lin(b, 4)
                if more:
                    project(it, b + 1, KS)
                copy_lin(b, 5)
                save_acc(it, b, 0)
                if more:
                    exp_min(b + 1, 0)
                copy_lin(b, 6)
                save_acc(it, b, 1)
                copy_lin(b, 7)
                save_acc(it, b, 2)
                if more:
                    project(it, b + 1, QS)
                save_acc(it, b, 3)
                save_T(it, 0)
                copy_maxima(it, 0)
                if more:
                    project(it, b + 1, QA)
                save_T(it, 1)
                if more:
                    project(it, b + 1, KA)
                save_T(it, 2)
                for i in range(NT + 8):
                    if more and i in (4, 7):
                        exp_min(b + 1, 1 + i // 7)
                    if i < NT:
                        wait_sc_full(act, b, ("exp", i))
                        if i < PA:
                            act.wait_ge(acc_full, b * N + (N_LIN - PA + i) // 2 + 1)
                        else:
                            act.wait_ge(pa_used, b * NT + i - PA + 1)
                        nc.scalar.activation(pa[(N_LIN + i) % PA], sc_of(("exp", i))[:, :], ACT.Exp)\
                            .then_inc(sc_drained[SC_SLOT["exp", i] % 2], 1)
                    if i == 0:
                        save_T(it, 3)
                        copy_maxima(it, 1)
                    for m in range(N):
                        if i == LAST_TILE[m] + LAG + 1:
                            save_acc(it, b, N + m)
                    for m in range(N):
                        if i == LAST_TILE[m] + LAG + 5:
                            save_T(it, N + m)
                    if not more and i == LAST_TILE[N - 1] + LAG + 2:
                        root(5, 0, B - 1)

            act.wait_ge(warm_ready, 1)
            nc.scalar.activation(warm[:, :], warm[:, :], ACT.Sqrt).then_inc(warm_ready, 1)
            root(1, 0, 1)
            for dst, src in early_cols:
                act.dma_start(dst, src.rearrange("(k p) -> p k", p=P), allow_slow_non_contiguous=True)\
                   .then_inc(early_loaded, 16)
            root(2, 0, 1)
            second_norm(1, 0, 1)
            act.wait_ge(early_loaded, EARLY_ALL)
            act.wait_ge(bias_ready, 2)
            start = ("start", 0)
            turned(start, 0)
            turned(start, 1)
            root(3, 1, B)
            project(start, 0, KS)
            project(start, 0, QS)
            for c in range(2):
                exp_min(0, c)
            project(start, 0, QA)
            project(start, 0, KA)
            for i in (QA, KA):
                use = Use(*start, f"p{i}")
                act.wait_ge(use.drained, use.count_drained)
                nc.scalar.activation(parts[i][:, 0, :], f[:, i, :], ACT.Copy).then_inc(part_copied, 1)
            for k, i in enumerate((QA, KA)):
                act.wait_ge(rest_ready, k + 1)
                nc.scalar.activation(parts[i][:, 1, :], rest[:, i, :], ACT.Copy).then_inc(part_copied, 1)
            act.wait_ge(pre_full, 2)
            for k in range(2):
                nc.scalar.activation(wpT[:, k, :], sc[k][:, 0:P], ACT.Copy).then_inc(sc_drained[k], 1)
            exp_min(0, 2)
            act.wait_ge(pre_full, 4)
            for k in range(2):
                nc.scalar.activation(w_mix[:, k, :], acc[k][:, 0:P], ACT.Copy).then_inc(acc_drained[k], 1)
            root(4, 1, B)

            with act.Fori(0, B - 1) as b:
                attend(("loop", b), b)
            attend(("end", B - 1), B - 1)

            def turned_quantised(t):
                act.wait_ge(pre_full, PRE_FULL + t + 1)
                width = P if t == 1 else L
                first = max(t - 1, 0) * L
                dst = wqT[:, :] if t == 1 else xqT_all[:, first:first + L]
                nc.scalar.activation(dst, sc[t % 2][:, 0:width // 2].bitcast(BF16), ACT.Copy)\
                    .then_inc(sc_drained[t % 2], 1)

            def gelus(b):
                act.wait_ge(sc_full, NSC * B + b)
                for k in range(FC):
                    act.wait_ge(misc_full, M_ALL + 6 * b + 2 + k)
                    nc.scalar.activation(hid[:, k, :], misc[(1 + k) % 2][:, :], ACT.Gelu, bias=b1c[:, k:k + 1])\
                        .then_inc(misc_drained[(1 + k) % 2], 1)

            for t in range(B):
                turned_quantised(t)
            root(6, B - 1, B)
            with act.Fori(0, B - 1) as b:
                gelus(b)
            turned_quantised(B)
            gelus(B - 1)

        @block.vector
        def _(dve):
            done = [0]
            base = [0]

            def step(ins):
                done[0] += 1
                ins.then_inc(dve_step, 1)
                dve.wait_ge(dve_step, base[0] + done[0])

            def rsqrt(tokens, j):
                nc.vector.tensor_scalar(var[:, tokens], mv[:, tokens, 1], LN_EPS, None, ALU.add).then_inc(var_ready, 1)
                rsqrt_end(tokens, j)

            def rsqrt_end(tokens, j):
                ve, root, r, t = var[:, tokens], sd[:, tokens], rs[:, tokens], rt[:, tokens]
                dve.wait_ge(sd_ready, j)
                step(nc.vector.reciprocal(r, root))
                step(nc.vector.tensor_tensor(t, r, r, ALU.mult))
                step(nc.vector.tensor_tensor(t, t, ve, ALU.mult))
                step(nc.vector.tensor_scalar(t, t, -0.5, 1.5, ALU.mult, ALU.add))
                step(nc.vector.tensor_tensor(r, r, t, ALU.mult))

            def stats(first, last, loads):
                for t in range(first * N, last * N):
                    if loads and t % N == 0:
                        dve.wait_ge(x_loaded[t // N], 16)
                    ins = nc.vector.bn_stats(st_all[:, t // N, t % N, :], xn_all[:, t // N, t % N, :])
                return ins

            def moments(first, last):
                for t in range(first * N, last * N):
                    ins = nc.vector.bn_aggr(mv[:, t, :], st_all[:, t // N, t % N, :])
                step(ins)

            def norm_batches(dst, first, last):
                for t in range(first * N, last * N):
                    ins = nc.vector.tensor_scalar(dst[:, t // N, t % N, :], xn_all[:, t // N, t % N, :],
                                                  mv[:, t, 0:1], rs[:, t:t + 1], ALU.subtract, ALU.mult)
                return ins

            def add_rows(it, name, v, o):
                use = Use(*it, name)
                dve.wait_ge(misc_full, use.count_full)
                row = b_nat[:, o:o + P].rearrange("p (h e) -> p h e", e=E)
                for n in range(N):
                    ins = nc.vector.tensor_tensor(v[:, n, :, 0:E],
                                                  use.bank[:, n * C:(n + 1) * C].rearrange("p (h e) -> p h e", e=E),
                                                  row, ALU.add)
                ins.then_inc(use.drained, 1)

            def split(i, src):
                step(nc.vector.tensor_copy(parts[i][:, 0, :], src))
                step(nc.vector.tensor_tensor(rest[:, i, :], src, parts[i][:, 0, :], ALU.subtract))
                step(nc.vector.tensor_copy(parts[i][:, 1, :], rest[:, i, :]))
                nc.vector.tensor_tensor(parts[i][:, 2, :], rest[:, i, :], parts[i][:, 1, :], ALU.subtract)\
                    .then_inc(parts_ready[i], 1)

            def elu_begin(it, c):
                if c < 2:
                    wait_misc_drained(dve, it, f"p{(KS, QS)[c]}")
                src = (f[:, KS, :], f[:, QS, :], k_lin[:, :])[c]
                nc.vector.tensor_scalar(phi[:, (1, 0, 2)[c], :], src, 0.0, None, ALU.min).then_inc(min_ready, 1)
                step(nc.vector.tensor_scalar(src, src, 0.0, ELU_SHIFT, ALU.max, ALU.add))

            def elu_end(b, c):
                src, dst = (f[:, KS, :], f[:, QS, :], k_lin[:, :])[c], phi[:, (1, 0, 2)[c], :]
                dve.wait_ge(exp_ready, 3 * b + c + 1)
                nc.vector.tensor_tensor(dst, dst, src, ALU.add).then_inc(phi_ready, 1)

            def split_linear(b, c):
                dve.wait_ge(phi_ready, 3 * b + c + 1)
                split((KS, QS)[c], phi[:, (1, 0)[c], :])

            def prepare_values(it):
                add_rows(it, "vs", v_s, P)
                use = Use(*it, "kn")
                dve.wait_ge(misc_full, use.count_full)
                nc.vector.tensor_tensor(k_lin[:, :].rearrange("p (n d) -> p n d", d=P),
                                        use.bank[:, :].rearrange("p (n d) -> p n d", d=P),
                                        b_nat[:, 2 * P:3 * P].rearrange("p (a d) -> p a d", a=1)
                                        .to_broadcast([P, N, P]), ALU.add).then_inc(use.drained, 1)
                dve.wait_ge(use.drained, use.count_drained)
                elu_begin(it, 2)

            def mask_window(b, i):
                wait_sc_drained(dve, b, ("exp", i))
                p = pa[(N_LIN + i) % PA].rearrange("p (h k) -> p h k", k=2 * C)
                nc.vector.tensor_tensor(p, p, window[:, :, :].rearrange("p (a w) r -> p a (w r)", a=1)
                                        .to_broadcast([P, 4, 2 * C]), ALU.min).then_inc(dve_masked, 1)

            def prepare_window(it, i):
                wait_misc_drained(dve, it, f"p{i}")
                split(i, f[:, i, :])

            def add_state(it, b, n):
                use = Use(*it, "kv12" if n else "kv0")
                dve.wait_ge(misc_full, use.count_full)
                o = 2 * P * (n // 2)
                m = use.bank[:, o:o + H * (E + 1)].rearrange("p (h f) -> p h f", h=H)
                if n == 0:
                    nc.vector.tensor_tensor(state[0][:, :, 0:E + 1], m, own_head[:, :, :], ALU.mult)\
                        .then_inc(use.drained, 1)
                else:
                    if n > 1:
                        dve.wait_ge(state_ready, 2 * b + n - 1)
                        nc.vector.tensor_tensor(kv_new[:, :, :], m, own_head[:, :, :], ALU.mult)\
                            .then_inc(use.drained, 1)
                        dve.wait_ge(use.drained, use.count_drained)
                    else:
                        step(nc.vector.tensor_tensor(kv_new[:, :, :], m, own_head[:, :, :], ALU.mult))
                        wait_misc_drained(dve, it, "kv0")
                    nc.vector.tensor_tensor(state[n][:, :, 0:E + 1], state[n - 1][:, :, 0:E + 1],
                                            kv_new[:, :, :], ALU.add).then_inc(state_ready, 1)

            def split_maxima(it):
                tokens = slice(L // 2, L)
                if it[0] == "end":
                    dve.wait_ge(c_copied, 1)
                else:
                    wait_misc_drained(dve, it, "cTb")
                step(nc.vector.tensor_copy(c_parts[:, 0, tokens], c_f[:, tokens]))
                step(nc.vector.tensor_tensor(c_rest[:, tokens], c_f[:, tokens], c_parts[:, 0, tokens], ALU.subtract))
                step(nc.vector.tensor_copy(c_parts[:, 1, tokens], c_rest[:, tokens]))
                nc.vector.tensor_tensor(c_parts[:, 2, tokens], c_rest[:, tokens], c_parts[:, 1, tokens],
                                        ALU.subtract).then_inc(c_ready[1], 1)

            def top(b, i):
                m, h0, nh = SOFT[i]
                wait_sc_full(dve, b, ("max", i))
                nc.vector.tensor_reduce(negc[:, m, h0:h0 + nh],
                                        sc_of(("max", i))[:, :].rearrange("p (h s) -> p h s", h=nh),
                                        AX_X, ALU.max, negate=True).then_inc(sc_drained[SC_SLOT["max", i] % 2], 1)

            def normalise(it, u):
                kind = u // N
                use = Use(*it, unit(u) + "nat")
                dve.wait_ge(misc_full, use.count_full)
                m = use.bank[:, :].rearrange("p (h f) -> p h f", f=VW)
                if kind == 0:
                    step(nc.vector.tensor_scalar(den[:, :], m[:, :, E], DEN_EPS, None, ALU.add))
                step(nc.vector.reciprocal(rden[:, :], m[:, :, E] if kind else den[:, :]))
                if u >= 2:
                    wait_misc_full(dve, it, unit(u - 2) + "T")
                nc.vector.tensor_tensor(nat[u % 2][:, :].rearrange("p (h e) -> p h e", e=E), m[:, :, 0:E],
                                        rden[:, :].rearrange("p (h a) -> p h a", a=1).to_broadcast([P, H, E]),
                                        ALU.mult).then_inc(use.drained, 1)

            rows = []

            def token_stats(first, last):
                for t in range(first, last):
                    ins = nc.vector.bn_stats(st_all[:, t // N, t % N, :], x1_all[:, t // N, t % N, :])
                step(ins)
                for t in range(first, last):
                    ins = nc.vector.bn_aggr(mv[:, t, :], st_all[:, t // N, t % N, :])
                step(ins)

            def norm_tokens(b):
                for n in range(N):
                    ins = nc.vector.tensor_scalar(hn[:, n, :], x1_all[:, b, n, :], mv[:, b * N + n, 0:1],
                                                  rs[:, bass.ds(b * N + n, 1)], ALU.subtract, ALU.mult)
                ins.then_inc(h_ready, 1)

            y, big = q_e[:, QS, :], q_e[:, KS, :]

            def quantise(k, dst, src, scale, w):
                if k:
                    dve.wait_ge(quantised, k)
                step(nc.vector.tensor_scalar(y[:, 0:w], src, scale, None, ALU.mult))
                step(nc.vector.tensor_scalar(big[:, 0:w].bitcast(I32), y[:, 0:w].bitcast(I32),
                                             EXPONENT_BITS, None, ALU.bitwise_and))
                step(nc.vector.tensor_scalar(big[:, 0:w], big[:, 0:w], FP8_MIN_NORMAL, FP8_ROUND,
                                             ALU.max, ALU.mult))
                step(nc.vector.tensor_tensor(y[:, 0:w], y[:, 0:w], big[:, 0:w], ALU.add))
                nc.vector.tensor_tensor(dst, y[:, 0:w], big[:, 0:w], ALU.subtract).then_inc(quantised, 1)

            def attend(it, b):
                more = it[0] == "loop"
                after = {4: 0, 6: 1, 9: 2, 12: 3}
                for i in range(NT):
                    top(b, i)
                    if i in after:
                        normalise(it, after[i])
                    if not more and i == 3:
                        nc.vector.tensor_reduce(am[:, 0:1], xn_all[:, :, :, :].rearrange("p b n d -> p (b n d)"),
                                                AX_X, ALU.max, apply_absolute_value=True)
                        nc.vector.tensor_reduce(am[:, 1:2], wf[:, :], AX_X, ALU.max, apply_absolute_value=True)\
                            .then_inc(amax_ready, 1)
                    if more:
                        if i == 0:
                            elu_begin(it, 0)
                        if i == 2:
                            elu_end(b + 1, 0)
                            split_linear(b + 1, 0)
                split_maxima(it)
                if more:
                    elu_begin(it, 1)
                    prepare_values(it)
                    elu_end(b + 1, 1)
                    mask_window(b, 5)
                    normalise(it, N)
                    elu_end(b + 1, 2)
                    split_linear(b + 1, 1)
                    mask_window(b, 8)
                    normalise(it, N + 1)
                    prepare_window(it, QA)
                    mask_window(b, 11)
                    prepare_window(it, KA)
                    normalise(it, N + 2)
                    add_rows(it, "va", v_a, 0)
                    normalise(it, N + 3)
                    for n in range(N - 1):
                        add_state(it, b + 1, n)
                else:
                    use = Use(*it, "cTb")
                    dve.wait_ge(misc_full, use.count_full)
                    nc.vector.tensor_reduce(am1[:, :], use.bank[0:1, 2 * P:4 * P].rearrange("p (a d) -> p a d", a=2),
                                            AX_X, ALU.max).then_inc(use.drained, 1)
                    dve.wait_ge(use.drained, use.count_drained)
                    nc.vector.tensor_scalar(am1[:, :], am1[:, :], AMAX_MIN, None, ALU.max).then_inc(amax_ready, 1)
                    token_stats(0, (B - 1) * N)
                    use = Use(*it, "amb")
                    dve.wait_ge(misc_full, use.count_full)
                    nc.vector.tensor_copy(amb[:, :], use.bank[:, 0:2]).then_inc(use.drained, 1)
                    dve.wait_ge(use.drained, use.count_drained)
                    step(nc.vector.reciprocal(amb[:, :], amb[:, :]))
                    step(nc.vector.tensor_scalar(fscale[:, :], amb[:, :], FP8_MAX, None, ALU.mult))
                    step(nc.vector.reciprocal(finv[:, :], fscale[:, :]))
                    step(nc.vector.tensor_tensor(dequant[:, :], finv[:, 0:1], finv[:, 1:2], ALU.mult))
                    rows[:] = [xn_all[:, t, :, :].rearrange("p n d -> p (n d)") for t in range(B)]
                    quantise(0, xq[:, 0, :], rows[0], fscale[:, 0:1], L)
                    normalise(it, N)
                    quantise(1, wq[:, :], wf[:, :], fscale[:, 1:2], P)
                    quantise(2, xq[:, 1, :], rows[1], fscale[:, 0:1], L)
                    normalise(it, N + 1)
                    quantise(3, xq[:, 2, :], rows[2], fscale[:, 0:1], L)
                    normalise(it, N + 2)
                    normalise(it, N + 3)
                    rsqrt(slice(0, (B - 1) * N), 5)
                    norm_tokens(0)
                use = Use(*it, "mix")
                dve.wait_ge(misc_full, use.count_full)
                step(nc.vector.tensor_tensor(x1_all[:, b, :, :], use.bank[:, :].rearrange("p (n d) -> p n d", d=P),
                                             xn_all[:, b, :, :], ALU.add))
                nc.vector.tensor_tensor(x1_all[:, b, :, :], x1_all[:, b, :, :],
                                        b_mix[:, :].rearrange("p (a d) -> p a d", a=1).to_broadcast([P, N, P]),
                                        ALU.add).then_inc(use.drained, 1)

            for j in (1, 2):
                step(stats(0, 1, j == 1))
                moments(0, 1)
                rsqrt(slice(0, N), j)
                if j == 1:
                    step(norm_batches(xn_all, 0, 1))
            nc.vector.scalar_tensor_tensor(out=shift[:, 0:N], in0=mv[:, 0:N, 0], scalar=-1.0,
                                           in1=rs[:, 0:N], op0=ALU.mult, op1=ALU.mult)\
                .then_inc(shift_ready, 1)
            dve.wait_ge(early_loaded, EARLY_ALL)
            nc.vector.tensor_scalar(gb[:, :], cols[:, 0:4], 1.0, None, ALU.mult).then_inc(bias_ready, 1)
            dve.wait_ge(bias_ready, 1)
            nc.vector.tensor_scalar(gb[:, 0:4:2], cols[:, 0:4:2], SCALE, None, ALU.mult).then_inc(bias_ready, 1)
            step(stats(1, B, True))
            moments(1, B)
            rsqrt(slice(N, B * N), 3)
            start = ("start", 0)
            elu_begin(start, 0)
            elu_begin(start, 1)
            step(norm_batches(xn_all, 1, B))
            dve.wait_ge(const_ready, CONST_EARLY)
            for c in range(2):
                elu_end(0, c)
                split_linear(0, c)
            prepare_values(start)
            step(stats(1, B, False))
            moments(1, B)
            others = slice(N, B * N)
            nc.vector.tensor_scalar(var[:, others], mv[:, others, 1], LN_EPS, None, ALU.add).then_inc(var_ready, 1)
            elu_end(0, 2)
            rsqrt_end(others, 4)
            dve.wait_ge(xh_ready, 1)
            norm_batches(xh_all, 1, 2).then_inc(xh_ready, 1)
            add_rows(start, "va", v_a, 0)
            add_state(start, 0, 0)
            dve.wait_ge(late_loaded, LATE_ALL)
            step(nc.vector.tensor_scalar(pre_col[:, :], cols[:, 8:9], cols[:, 9:10], None, ALU.add))
            nc.vector.tensor_scalar(pre, ones[:, :], pre_col[:, :], None, ALU.mult).then_inc(pre_ready, 1)
            for n in range(1, N - 1):
                add_state(start, 0, n)
            use = Use(*start, "pre")
            dve.wait_ge(misc_full, use.count_full)
            nc.vector.tensor_tensor(b_mix[:, :], use.bank[:, 0:P], bo_rows, ALU.add).then_inc(use.drained, 1)
            for b in range(2, B):
                norm_batches(xh_all, b, b + 1).then_inc(xh_ready, 1)
            before = done[0]
            LOOP_STEPS = 3 + 3 + 12 + 1 + 3 * N + 1
            done[0] = 0
            with dve.Fori(0, B - 1) as b:
                base[0] = b * LOOP_STEPS + before
                attend(("loop", b), b)
            assert done[0] == LOOP_STEPS
            base[0] = 0
            done[0] = before + (B - 1) * LOOP_STEPS
            attend(("end", B - 1), B - 1)

            def norm_columns(bank, count):
                dve.wait_ge(misc_full, count)
                nc.vector.tensor_scalar(hT[:, :], misc[bank][:, :], cols[:, 6:7], cols[:, 7:8], ALU.mult, ALU.add)\
                    .then_inc(misc_drained[bank], 1)

            def sums(b, bank, full):
                dve.wait_ge(sc_drained[1], SC_MLP + b)
                dve.wait_ge(misc_full, full)
                nc.vector.scalar_tensor_tensor(out=r1, in0=misc[bank][:, :], scalar=dequant[:, 0:1],
                                               in1=x1_all[:, b, :, :].rearrange("p n d -> p (n d)"),
                                               op0=ALU.mult, op1=ALU.add).then_inc(misc_drained[bank], 1)
                dve.wait_ge(resid_ready, b + 1)
                dve.wait_ge(sc_full, NSC * B + b + 1)
                nc.vector.tensor_tensor(o_sb[:, :], sc[1][:, 0:512], r2, ALU.add).then_inc(sc_drained[1], 1)

            wait_misc_drained(dve, ("end", B - 1), "mix")
            token_stats((B - 1) * N, B * N)
            last_tokens = slice((B - 1) * N, B * N)
            nc.vector.tensor_scalar(var[:, last_tokens], mv[:, last_tokens, 1], LN_EPS, None, ALU.add)\
                .then_inc(var_ready, 1)
            norm_columns(0, M_ALL + 1)
            rsqrt_end(last_tokens, 6)
            quantise(4, xq[:, 3, :], rows[3], fscale[:, 0:1], L)
            with dve.Fori(0, B - 1) as b:
                norm_tokens(b + 1)
                norm_columns(1, M_ALL + 6 * b + 6)
                sums(b, 0, M_ALL + 6 * b + 7)
            sums(B - 1, 1, M_ALL + 6 * B)

        @block.tensor
        def _(pe):
            def open_misc(it, name):
                use = Use(*it, name)
                if it[0] != "start" or use.count_open > 0:
                    pe.wait_ge(use.drained, use.count_open)
                return use.bank

            def open_sc(b, use):
                u = SC_SLOT[use]
                pe.wait_ge(sc_drained[u % 2], b * (NSC // 2) + u // 2 + 1)
                return sc[u % 2]

            def open_acc(b, u):
                pe.wait_ge(acc_drained[u % 2], b * (N_ACC // 2) + u // 2 + 1)
                return acc[u % 2]

            def turn(it, b, k):
                if k == 0:
                    if it[0] == "start":
                        pe.wait_ge(xh_ready, 1)
                    else:
                        pe.wait_ge(xh_loaded, 16 * b)
                m = open_misc(it, ("xTa", "xTb")[k])
                for n in range(N // 2):
                    ins = nc.tensor.transpose(m[:, n * C:(n + 1) * C], xh[:, k * N // 2 + n, :], ident[:, :])
                ins.then_inc(misc_full, 1)

            def project(it, i):
                m = open_misc(it, f"p{i}")
                nc.tensor.matmul(m[:, :], w_cols[:, i, :], xT[:, :], start=True, stop=True).then_inc(misc_full, 1)

            def natural(it, name, o):
                m = open_misc(it, name)
                for n in range(N):
                    ins = nc.tensor.matmul(m[:, n * C:(n + 1) * C], xT[:, n * C:(n + 1) * C], w_nat[:, o:o + P],
                                           start=True, stop=True)
                ins.then_inc(misc_full, 1)

            def key_values(it, b, n):
                if n == 0:
                    pe.wait_ge(phi_ready, 3 * (b + 1))
                m = open_misc(it, "kv12" if n else "kv0")
                for c in range(n, 2 * n + 1):
                    o = 2 * P * (c // 2)
                    ins = nc.tensor.matmul(m[:, o:o + H * (E + 1)], phi[:, 2, c * C:(c + 1) * C],
                                           v_s[:, c, :, 0:E + 1], start=True, stop=True)
                ins.then_inc(misc_full, 1)

            def lin_scores(b, t):
                dst = open_sc(b, ("lin", t))
                n, h0 = t // 2, 8 * (t % 2)
                for hh in range(8):
                    ins = nc.tensor.matmul(dst[:, hh * C:(hh + 1) * C],
                                           stack[KS][0:KPAD, h0 + hh, n * C:(n + 1) * C],
                                           stack[QS][0:KPAD, h0 + hh, n * C:(n + 1) * C], start=True, stop=True)
                ins.then_inc(sc_full, 1)

            def max_scores(b, i):
                mc, h0, nh = SOFT[i]
                t = open_sc(b, ("max", i))
                w = 1024 // nh
                mask = mask_first[:, :, :] if mc == 0 else mask_win[:, :, :, :]
                for bank in range(2):
                    nc.tensor.matmul(t[:, bank * 512:(bank + 1) * 512], ident16[:, :], mask,
                                     start=True, stop=False, skip_group_check=True)
                    for hh in range(nh // 2):
                        hl = bank * nh // 2 + hh
                        ins = nc.tensor.matmul(t[:, hl * w:(hl + 1) * w],
                                               stack[QA][0:KPAD, h0 + hl, mc * C:(mc + 1) * C],
                                               stack[KA][0:KPAD, h0 + hl, (mc + 1) * C - w:(mc + 1) * C],
                                               start=False, stop=True, skip_group_check=True)
                ins.then_inc(sc_full, 1)

            def exp_scores(b, i):
                mc, h0, nh = SOFT[i]
                t = open_sc(b, ("exp", i))
                half = 8 // nh
                for hh in range(nh):
                    for w in range(half):
                        key = (mc - half + 1 + w) * C
                        o = (hh * half + w) * C
                        ins = nc.tensor.matmul(t[:, o:o + C], stack[KA][0:KPAD + CROWS, h0 + hh, key:key + C],
                                               stack[QA][0:KPAD + CROWS, h0 + hh, mc * C:(mc + 1) * C],
                                               start=True, stop=True)
                ins.then_inc(sc_full, 1)

            def lin_out(b, n):
                a = open_acc(b, n)
                for g in range(4):
                    cols_g = slice(g * C, (g + 1) * C)
                    if n:
                        pe.wait_ge(state_ready, 2 * b + max(n - 1, 1))
                        nc.tensor.matmul(a[:, cols_g], state[n - 1][:, 4 * g:4 * g + 4, :],
                                         phi[:, 0, n * C:(n + 1) * C], start=(g == 0), stop=False,
                                         skip_group_check=True)
                    t = 2 * n + g // 2
                    if g % 2 == 0:
                        pe.wait_ge(lin_masked, b * N_LIN + t + 1)
                    for j in range(4):
                        ins = nc.tensor.matmul(a[32 * j:32 * j + VW, cols_g], v_s[:, n, 4 * g + j, :],
                                               pa[t % PA][:, (4 * (g % 2) + j) * C:(4 * (g % 2) + j + 1) * C],
                                               start=(n == 0 and g == 0), stop=True, skip_group_check=True)
                ins.then_inc(acc_full, 1)

            def window_out(b, i, more):
                mc, h0, nh = SOFT[i]
                a = open_acc(b, N + mc) if h0 == 0 else acc[(N + mc) % 2]
                if more and i in DVE_MASKS:
                    pe.wait_ge(dve_masked, b * len(DVE_MASKS) + DVE_MASKS.index(i) + 1)
                else:
                    before = i - sum(j < i for j in DVE_MASKS) if more else i
                    pe.wait_ge(masked, b * (NT - len(DVE_MASKS)) + before + 1)
                half = 8 // nh
                p = pa[(N_LIN + i) % PA]
                for g in range(nh // 4):
                    for w in range(half):
                        for j in range(4):
                            hh = 4 * g + j
                            o = (hh * half + w) * C
                            gg = (h0 + hh) // 4
                            ins = nc.tensor.matmul(
                                a[32 * j:32 * j + VW, gg * C:(gg + 1) * C],
                                v_a[:, mc - half + 1 + w, h0 + hh, :], p[:, o:o + C],
                                start=(gg == 0 and w == 0), stop=(w == half - 1), skip_group_check=True)
                ins.then_inc(pa_used, 1)

            def to_tokens(it, b, u):
                m = open_misc(it, unit(u) + "nat")
                pe.wait_ge(acc_drained[u % 2], b * (N_ACC // 2) + u // 2 + 2)
                for g in range(4):
                    ins = nc.tensor.transpose(m[:, g * C:(g + 1) * C], acc_s[u % 2][:, g * C:(g + 1) * C],
                                              ident[:, :])
                ins.then_inc(misc_full, 1)

            def to_columns(it, u):
                m = open_misc(it, unit(u) + "T")
                wait_misc_drained(pe, it, unit(u) + "nat")
                nc.tensor.transpose(m[:, 0:C], nat[u % 2][:, :], ident[:, :]).then_inc(misc_full, 1)

            def turn_maxima(it, half):
                if half:
                    wait_sc_drained(pe, it[1], ("max", NT - 2))
                    wait_sc_drained(pe, it[1], ("max", NT - 1))
                m = open_misc(it, ("cTa", "cTb")[half])
                for n in range(N // 2):
                    ins = nc.tensor.transpose(m[0:H, n * C:(n + 1) * C], negc[:, half * N // 2 + n, :], ident[:, :])
                if half and it[0] == "end":
                    pe.wait_ge(amax_ready, 1)
                    for k in range(2):
                        ins = nc.tensor.transpose(m[0:1, (2 + k) * P:(3 + k) * P], am[:, k:k + 1], ident[:, :])
                ins.then_inc(misc_full, 1)

            def attend(it, b):
                more = it[0] == "loop"
                for i in (KS, QS):
                    pe.wait_ge(stacked[i], 16 * len(RUNS) * (b + 1))
                for t in range(PA):
                    lin_scores(b, t)
                    if more and t in (1, 3):
                        turn(it, b + 1, t // 2)
                lin_out(b, 0)
                for i in (QA, KA):
                    pe.wait_ge(stacked[i], 16 * len(RUNS) * (b + 1))
                for i in range(NT):
                    max_scores(b, i)
                    if PA + i < N_LIN:
                        lin_scores(b, PA + i)
                    if more and i == 0:
                        wait_misc_drained(pe, it, "xTa")
                        wait_misc_drained(pe, it, "xTb")
                        project(it, KS)
                    if i in (1, 2, 5):
                        lin_out(b, {1: 1, 2: 2, 5: 3}[i])
                    if i in (3, 5, 9, 11):
                        to_tokens(it, b, {3: 0, 5: 1, 9: 2, 11: 3}[i])
                    if more and i == 3:
                        project(it, QS)
                    if i == 7:
                        to_columns(it, 0)
                    if i == 8:
                        turn_maxima(it, 0)
                    if more and i == 8:
                        project(it, QA)
                    if i in (10, 12):
                        to_columns(it, {10: 1, 12: 2}[i])
                    if more and i == 10:
                        project(it, KA)
                pe.wait_ge(c_stacked[0], 16 * CROWS * (b + 1))
                for i in range(NT + LAG + 6):
                    if i == LAST_TILE[1] + 1:
                        pe.wait_ge(c_stacked[1], 16 * CROWS * (b + 1))
                    if i < NT:
                        exp_scores(b, i)
                    if i == 0:
                        to_columns(it, N - 1)
                        turn_maxima(it, 1)
                    if more and i in (0, 1):
                        natural(it, *(("vs", P), ("kn", 2 * P))[i])
                    if LAG <= i < NT + LAG:
                        window_out(b, i - LAG, more)
                    if more and i == NT + LAG:
                        natural(it, "va", 0)
                    for mc in range(N):
                        if i == LAST_TILE[mc] + LAG + 2:
                            to_tokens(it, b, N + mc)
                        if i == LAST_TILE[mc] + LAG + 4:
                            to_columns(it, N + mc)
                    if not more and i == LAST_TILE[0] + LAG:
                        pe.wait_ge(amax_ready, 2)
                        m = open_misc(it, "amb")
                        nc.tensor.matmul(m[:, 0:2], ones[0:1, :], am1[:, :], start=True, stop=True)\
                            .then_inc(misc_full, 1)
                    if more and i == NT + LAG + 2:
                        key_values(it, b + 1, 0)
                if more:
                    key_values(it, b + 1, 1)
                m = open_misc(it, "mix")
                wait_misc_drained(pe, it, f"s{N - 1}T")
                for n in range(N):
                    pe_cols = slice(n * C, (n + 1) * C)
                    nc.tensor.matmul(m[:, pe_cols], oT[:, 0, pe_cols], w_mix[:, 1, :], start=True, stop=False)
                    ins = nc.tensor.matmul(m[:, pe_cols], oT[:, 1, pe_cols], w_mix[:, 0, :], start=False, stop=True)
                ins.then_inc(misc_full, 1)

            pe.wait_ge(ident_ready, 1)
            pe.wait_ge(early_loaded, EARLY_ALL)
            start = ("start", 0)
            turn(start, 0, 0)
            turn(start, 0, 1)
            wait_misc_drained(pe, start, "xTa")
            wait_misc_drained(pe, start, "xTb")
            project(start, KS)
            project(start, QS)
            project(start, QA)
            project(start, KA)
            natural(start, "vs", P)
            natural(start, "kn", 2 * P)
            pe.wait_ge(late_loaded, LATE_ALL)
            for k in range(2):
                nc.tensor.transpose(sc[k][:, 0:P], wp[:, k, :], ident[:, :]).then_inc(pre_full, 1)
            natural(start, "va", 0)
            for k in range(2):
                pe.wait_ge(sc_drained[k], 1)
                nc.tensor.matmul(acc[k][:, 0:P], wpT[:, k, :], wo[:, :], start=True, stop=True).then_inc(pre_full, 1)
            pe.wait_ge(const_ready, CONST_ALL)
            for n in range(2):
                key_values(start, 0, n)
            m = open_misc(start, "pre")
            pe.wait_ge(pre_ready, 1)
            nc.tensor.matmul(m[:, 0:P], pre, wo[:, :], start=True, stop=True).then_inc(misc_full, 1)

            with pe.Fori(0, B - 1) as b:
                attend(("loop", b), b)
            attend(("end", B - 1), B - 1)

            def turn_tokens(b, bank, opened):
                pe.wait_ge(h_ready, b + 1)
                pe.wait_ge(misc_drained[bank], opened)
                for n in range(N):
                    ins = nc.tensor.transpose(misc[bank][:, n * C:(n + 1) * C], hn[:, n, :], ident[:, :])
                ins.then_inc(misc_full, 1)

            def turn_quantised(t):
                pe.wait_ge(quantised, t + 1)
                pe.wait_ge(sc_drained[t % 2], 1 + B * (NSC // 2) + t // 2)
                turned = sc[t % 2][:, 0:256].bitcast(BF16)
                if t == 1:
                    ins = nc.tensor.transpose(turned[:, 0:P], wq[:, :], ident16[:, :])
                else:
                    for n in range(N):
                        ins = nc.tensor.transpose(turned[:, n * C:(n + 1) * C],
                                                  xq[:, max(t - 1, 0), n * C:(n + 1) * C], ident16[:, :])
                ins.then_inc(pre_full, 1)

            def mlp(b, more):
                half = b * 3 + M_ALL // 2
                for k in range(FC):
                    bank = (k + 1) % 2
                    pe.wait_ge(misc_drained[bank], half + (k + 1) // 2)
                    nc.tensor.matmul(misc[bank][:, :], w1[:, k * P:(k + 1) * P], hT[:, :], start=True, stop=True)\
                        .then_inc(misc_full, 1)
                if more:
                    turn_tokens(b + 1, 1, half + 2)
                bank, opened = (0, half + 3) if more else (1, half + 2)
                pe.wait_ge(misc_drained[bank], opened)
                for n in range(N):
                    ins = nc.tensor.matmul(misc[bank][:, n * C:(n + 1) * C], xqT_all[:, bass.ds(b * L + n * C, C)],
                                           wqT[:, :], start=True, stop=True)
                ins.then_inc(misc_full, 1)
                pe.wait_ge(misc_drained[0], half + 3)
                pe.wait_ge(sc_drained[1], SC_MLP + b)
                for n in range(N):
                    for k in range(FC):
                        ins = nc.tensor.matmul(sc[1][:, n * C:(n + 1) * C], hid[:, k, n * C:(n + 1) * C],
                                               w2[:, k, :], start=(k == 0), stop=(k == FC - 1))
                ins.then_inc(sc_full, 1)

            turn_tokens(0, 0, M_ALL // 2)
            for t in range(B):
                turn_quantised(t)
            pe.wait_ge(sc_drained[0], SC_MLP)
            pe.wait_ge(sc_drained[1], SC_MLP)
            pe.wait_ge(misc_drained[0], M_ALL // 2 + 1)
            with pe.Fori(0, B - 1) as b:
                mlp(b, True)
            turn_quantised(B)
            pe.wait_ge(sc_drained[0], SC_MLP + 1)
            mlp(B - 1, False)


_INS = ["x", "g1", "b1", "Wqkv_a", "bqkv_a", "Wp_a", "bp_a", "Wqkv_s", "bqkv_s", "Wo_s", "bo_s", "Wo", "bo",
        "gm", "bm", "W1", "b1m", "W2", "b2m"]
_INS = ["L0_attn_" + n for n in _INS] + ["L0_ffn_weight", "L0_ffn_bias"]


def kernel(**inputs):
    import numpy as _np
    import concourse.bacc as _bacc
    from concourse.bass_utils import run_bass_kernel_spmd as _run

    nc = _bacc.Bacc("TRN2", target_bir_lowering=False, num_devices=1)
    arrays, args = {}, []
    for name in _INS:
        a = _np.ascontiguousarray(inputs[name])
        arrays[name] = a
        args.append(nc.dram_tensor(name, a.shape, F32, kind="ExternalInput").ap())
    shape = arrays["L0_attn_x"].shape
    args.append(nc.dram_tensor("out", shape, F32, kind="ExternalOutput").ap())
    attention_block_kernel(nc, *args)
    r = _run(nc, [arrays], core_ids=[0])
    return r.results[0]["out"]
```
